# Optimizing a Trainium2 kernel written in Bass

```python
import numpy as np
import jax
import jax.numpy as jnp

def _softmax(x, axis=-1):
    return jax.nn.softmax(x, axis=axis)

def _gelu(x):
    return jax.nn.gelu(x, approximate=True)

def _silu(x):
    return jax.nn.silu(x)

def _sigmoid(x):
    return jax.nn.sigmoid(x)

def _layernorm(x, axis=-1, eps=1e-05):
    m = jnp.mean(x, axis=axis, keepdims=True)
    v = jnp.var(x, axis=axis, keepdims=True)
    return (x - m) / jnp.sqrt(v + eps)

def _scatter_add(tgt, idx, src, axis=0):
    return tgt.at[idx].add(src)

def _segment_sum(src, seg, n):
    return jax.ops.segment_sum(src, seg, n)
kernel_name = 'mk_xattn_ffn_d2_seqx_r4_175231'

def setup_inputs(seed: int=0):
    np.random.seed(seed)
    _w = jnp.asarray

    def _rec_inputs():
        import jax
        import jax.numpy as jnp
        _rk = jax.random.key(seed)
        x = -0.0003929 + 0.9999 * jax.random.normal(jax.random.fold_in(_rk, 1), (8, 100, 256), jnp.float32)
        _lenS = 100 - jax.random.randint(jax.random.fold_in(_rk, 7), (8,), 0, max(1, 100 // 4) + 1, jnp.int32)
        _lenS2 = 361 - jax.random.randint(jax.random.fold_in(_rk, 8), (8,), 0, max(1, 361 // 4) + 1, jnp.int32)
        _ctx_1024P = jax.random.normal(jax.random.fold_in(_rk, 11), (8, 16, 256), jnp.float32)
        _ctx_1024c = jax.random.dirichlet(jax.random.fold_in(_rk, 511), 0.3 * jnp.ones((16,), jnp.float32), (8, 361))
        _ctx_1024t = jnp.einsum('bsk,bkd->bsd', _ctx_1024c, _ctx_1024P)
        _ctx_1024t = _ctx_1024t * jax.lax.rsqrt(jnp.mean(jnp.square(_ctx_1024t)) + 1e-12) * 0.953939
        ctx_1024 = 2.81802e-05 + 1.00001 * (_ctx_1024t + 0.3 * jax.random.normal(jax.random.fold_in(_rk, 611), (8, 361, 256), jnp.float32))
        return (x, ctx_1024)
    x, ctx_1024 = _rec_inputs()

    def _L0_xattn_setup():
        import jax, jax.numpy as jnp
        import numpy as np
        B, T, C, H = (4, 1024, 256, 16)
        D = C // H

        def _heads(t):
            b, n, c = t.shape
            return t.reshape(b, n, H, D).transpose(0, 2, 1, 3)
        key = jax.random.key(seed)
        ks = jax.random.split(key, 10)
        s = 1.0 / np.sqrt(C)
        return {'x': jax.random.normal(ks[0], (B, T, C), jnp.float32), 'y': jax.random.normal(ks[1], (B, T, C), jnp.float32), 'Wq': jax.random.normal(ks[2], (C, C), jnp.float32) * s, 'bq': jnp.zeros((C,), jnp.float32), 'Wk': jax.random.normal(ks[3], (C, C), jnp.float32) * s, 'bk': jnp.zeros((C,), jnp.float32), 'Wv': jax.random.normal(ks[4], (C, C), jnp.float32) * s, 'bv': jnp.zeros((C,), jnp.float32), 'Wp': jax.random.normal(ks[5], (C, C), jnp.float32) * s, 'bp': jnp.zeros((C,), jnp.float32)}
    _L0_xattn_all = _L0_xattn_setup()
    _L0_xattn_in = {k: v for k, v in _L0_xattn_all.items() if k in ('Wq', 'bq', 'Wk', 'bk', 'Wv', 'bv', 'Wp', 'bp')}
    del _L0_xattn_all

    def _L0_ffn_setup():
        import jax, jax.numpy as jnp
        import numpy as np
        LN_EPS = 1e-05

        def _swiglu(h, w_gate_up, w_down):
            gu = h @ w_gate_up.T
            gate, up = jnp.split(gu, 2, axis=-1)
            return jax.nn.silu(gate) * up @ w_down.T
        key = jax.random.key(seed)
        ks = jax.random.split(key, 6)
        d_model, d_ff, E = (256, 1024, 8)
        shared_d_ff = d_ff // 4
        routed_d_ff = d_ff - shared_d_ff
        B, S = (4, 512)
        x = jax.random.normal(ks[0], (B, S, d_model), dtype=jnp.float32)
        ln_gamma = jnp.ones((d_model,), jnp.float32)
        ln_beta = jnp.zeros((d_model,), jnp.float32)
        router_w = jax.random.normal(ks[1], (E, d_model), jnp.float32) * 0.02
        gate_up_w = jax.random.normal(ks[2], (E, 2 * routed_d_ff, d_model), jnp.float32) * (1.0 / np.sqrt(d_model))
        down_w = jax.random.normal(ks[3], (E, d_model, routed_d_ff), jnp.float32) * (1.0 / np.sqrt(routed_d_ff))
        shared_gate_up_w = jax.random.normal(ks[4], (2 * shared_d_ff, d_model), jnp.float32) * (1.0 / np.sqrt(d_model))
        shared_down_w = jax.random.normal(ks[5], (d_model, shared_d_ff), jnp.float32) * (1.0 / np.sqrt(shared_d_ff))
        return dict(x=x, ln_gamma=ln_gamma, ln_beta=ln_beta, router_w=router_w, gate_up_w=gate_up_w, down_w=down_w, shared_gate_up_w=shared_gate_up_w, shared_down_w=shared_down_w)
    _L0_ffn_all = _L0_ffn_setup()
    _L0_ffn_in = {k: v for k, v in _L0_ffn_all.items() if k in ('ln_gamma', 'ln_beta', 'router_w', 'gate_up_w', 'down_w', 'shared_gate_up_w', 'shared_down_w')}
    del _L0_ffn_all

    def _L1_xattn_setup():
        import jax, jax.numpy as jnp
        import numpy as np
        B, S1, S2, E, P = (8, 512, 512, 256, 256)
        key = jax.random.key(seed)
        k1, k2, k3, k4, k5 = jax.random.split(key, 5)
        query = jax.random.normal(k1, (B, S1, E), dtype=jnp.float32)
        key_t = jax.random.normal(k2, (B, S2, E), dtype=jnp.float32)
        value = jax.random.normal(k3, (B, S2, E), dtype=jnp.float32)
        bound = 1.0 / np.sqrt(E)
        W = jax.random.uniform(k4, (P, E), minval=-bound, maxval=bound, dtype=jnp.float32)
        b = jax.random.uniform(k5, (P,), minval=-bound, maxval=bound, dtype=jnp.float32)
        return {'query': query, 'key': key_t, 'value': value, 'W': W, 'b': b}
    _L1_xattn_all = _L1_xattn_setup()
    _L1_xattn_in = {k: v for k, v in _L1_xattn_all.items() if k in ('W', 'b')}
    del _L1_xattn_all

    def _L1_ffn_setup():
        import math
        import jax, jax.numpy as jnp
        import numpy as np
        NUM_EXPERTS = 8
        CAPACITY_FACTOR = 1.5
        key = jax.random.key(seed)
        ks = jax.random.split(key, 4)
        B, T, D, F, E = (4, 512, 256, 1024, NUM_EXPERTS)
        scale = 0.02
        return {'x': jax.random.normal(ks[0], (B, T, D), dtype=jnp.float32), 'router_w': jax.random.normal(ks[1], (E, D), dtype=jnp.float32) * scale, 'w1': jax.random.normal(ks[2], (E, D, F), dtype=jnp.float32) * scale, 'b1': jnp.zeros((E, F), dtype=jnp.float32), 'w2': jax.random.normal(ks[3], (E, F, D), dtype=jnp.float32) * scale, 'b2': jnp.zeros((E, D), dtype=jnp.float32)}
    _L1_ffn_all = _L1_ffn_setup()
    _L1_ffn_in = {k: v for k, v in _L1_ffn_all.items() if k in ('router_w', 'w1', 'b1', 'w2', 'b2')}
    del _L1_ffn_all
    return {'x': x, 'ctx_1024': ctx_1024, 'L0_xattn_Wq': _L0_xattn_in['Wq'], 'L0_xattn_bq': _L0_xattn_in['bq'], 'L0_xattn_Wk': _L0_xattn_in['Wk'], 'L0_xattn_bk': _L0_xattn_in['bk'], 'L0_xattn_Wv': _L0_xattn_in['Wv'], 'L0_xattn_bv': _L0_xattn_in['bv'], 'L0_xattn_Wp': _L0_xattn_in['Wp'], 'L0_xattn_bp': _L0_xattn_in['bp'], 'L0_ffn_ln_gamma': _L0_ffn_in['ln_gamma'], 'L0_ffn_ln_beta': _L0_ffn_in['ln_beta'], 'L0_ffn_router_w': _L0_ffn_in['router_w'], 'L0_ffn_gate_up_w': _L0_ffn_in['gate_up_w'], 'L0_ffn_down_w': _L0_ffn_in['down_w'], 'L0_ffn_shared_gate_up_w': _L0_ffn_in['shared_gate_up_w'], 'L0_ffn_shared_down_w': _L0_ffn_in['shared_down_w'], 'L1_xattn_W': _L1_xattn_in['W'], 'L1_xattn_b': _L1_xattn_in['b'], 'L1_ffn_router_w': _L1_ffn_in['router_w'], 'L1_ffn_w1': _L1_ffn_in['w1'], 'L1_ffn_b1': _L1_ffn_in['b1'], 'L1_ffn_w2': _L1_ffn_in['w2'], 'L1_ffn_b2': _L1_ffn_in['b2']}

def reference(x, ctx_1024, L0_xattn_Wq, L0_xattn_bq, L0_xattn_Wk, L0_xattn_bk, L0_xattn_Wv, L0_xattn_bv, L0_xattn_Wp, L0_xattn_bp, L0_ffn_ln_gamma, L0_ffn_ln_beta, L0_ffn_router_w, L0_ffn_gate_up_w, L0_ffn_down_w, L0_ffn_shared_gate_up_w, L0_ffn_shared_down_w, L1_xattn_W, L1_xattn_b, L1_ffn_router_w, L1_ffn_w1, L1_ffn_b1, L1_ffn_w2, L1_ffn_b2):
    import jax
    import jax.numpy as jnp

    def _L0_xattn_ref(x, y, Wq, bq, Wk, bk, Wv, bv, Wp, bp):
        import jax, jax.numpy as jnp
        import numpy as np
        B, T, C, H = (4, 1024, 256, 16)
        D = C // H

        def _heads(t):
            b, n, c = t.shape
            return t.reshape(b, n, H, D).transpose(0, 2, 1, 3)
        q = jax.nn.softmax(_heads(x @ Wq.T + bq), axis=-1)
        k = jax.nn.softmax(_heads(y @ Wk.T + bk), axis=-1)
        v = _heads(y @ Wv.T + bv)
        k_cumsum = jnp.sum(k, axis=-2, keepdims=True)
        D_inv = 1.0 / jnp.sum(q * k_cumsum, axis=-1, keepdims=True)
        kv = jnp.einsum('bhnd,bhne->bhde', k, v)
        out = q + jnp.einsum('bhnd,bhde->bhne', q, kv) * D_inv
        out = out.transpose(0, 2, 1, 3).reshape(x.shape[0], x.shape[1], C)
        return out @ Wp.T + bp

    def _L0_ffn_ref(x, ln_gamma, ln_beta, router_w, gate_up_w, down_w, shared_gate_up_w, shared_down_w):
        import jax, jax.numpy as jnp
        import numpy as np
        LN_EPS = 1e-05

        def _swiglu(h, w_gate_up, w_down):
            gu = h @ w_gate_up.T
            gate, up = jnp.split(gu, 2, axis=-1)
            return jax.nn.silu(gate) * up @ w_down.T
        B, S, D = x.shape
        E = router_w.shape[0]
        top_k = 2
        xt = x.reshape(-1, D)
        mu = jnp.mean(xt, axis=-1, keepdims=True)
        var = jnp.mean(jnp.square(xt - mu), axis=-1, keepdims=True)
        normed = (xt - mu) * jax.lax.rsqrt(var + LN_EPS) * ln_gamma + ln_beta
        logits = normed.astype(jnp.float32) @ router_w.T
        probs = jax.nn.softmax(logits, axis=-1)
        top_v, top_i = jax.lax.top_k(probs, top_k)
        gates = jax.nn.softmax(top_v, axis=-1)
        comb = jnp.sum(jax.nn.one_hot(top_i, E, dtype=gates.dtype) * gates[..., None], axis=1)
        out = jnp.zeros_like(normed)
        for e in range(E):
            y = _swiglu(normed, gate_up_w[e], down_w[e])
            out = out + comb[:, e, None] * y
        out = out + _swiglu(normed, shared_gate_up_w, shared_down_w)
        return out.reshape(B, S, D)

    def _L1_xattn_ref(query, key, value, W, b):
        import jax, jax.numpy as jnp
        import numpy as np
        B, S1, S2, E, P = (8, 512, 512, 256, 256)
        q = jnp.einsum('bse,pe->bsp', query, W) + b
        k = jnp.einsum('bse,pe->bsp', key, W) + b
        v = jnp.einsum('bse,pe->bsp', value, W) + b
        scale = 1.0 / jnp.sqrt(jnp.float32(k.shape[-1]))
        scores = jnp.einsum('bqp,bkp->bqk', q, k) * scale
        weights = jax.nn.softmax(scores, axis=-1)
        return jnp.einsum('bqk,bkp->bqp', weights, v)

    def _L1_ffn_ref(x, router_w, w1, b1, w2, b2):
        import math
        import jax, jax.numpy as jnp
        import numpy as np
        NUM_EXPERTS = 8
        CAPACITY_FACTOR = 1.5
        B, T, D = x.shape
        E = router_w.shape[0]
        N = B * T
        C = max(math.ceil(CAPACITY_FACTOR * N / E), 1)
        x_flat = x.reshape(N, D)
        logits = x_flat @ router_w.T
        probs = jax.nn.softmax(logits, axis=-1)
        chosen_e = jnp.argmax(probs, axis=-1)
        chosen_p = jnp.max(probs, axis=-1)
        onehot = jax.nn.one_hot(chosen_e, E, dtype=jnp.float32)
        pos = jnp.take_along_axis(jnp.cumsum(onehot, axis=0), chosen_e[:, None], axis=1)[:, 0] - 1.0
        pos = pos.astype(jnp.int32)
        kept = pos < C
        pos_c = jnp.clip(pos, 0, C - 1)
        buf = jnp.zeros((E, C, D), dtype=x.dtype).at[chosen_e, pos_c].add(x_flat * kept[:, None].astype(x.dtype))
        h = jax.nn.gelu(jnp.einsum('ecd,edf->ecf', buf, w1) + b1[:, None, :], approximate=False)
        eo = jnp.einsum('ecf,efd->ecd', h, w2) + b2[:, None, :]
        y = eo[chosen_e, pos_c] * (chosen_p * kept.astype(x.dtype))[:, None]
        return y.reshape(B, T, D)
    x = x + _L0_xattn_ref(_layernorm(x, axis=-1), ctx_1024, L0_xattn_Wq, L0_xattn_bq, L0_xattn_Wk, L0_xattn_bk, L0_xattn_Wv, L0_xattn_bv, L0_xattn_Wp, L0_xattn_bp)
    x = x + _L0_ffn_ref(_layernorm(x, axis=-1), L0_ffn_ln_gamma, L0_ffn_ln_beta, L0_ffn_router_w, L0_ffn_gate_up_w, L0_ffn_down_w, L0_ffn_shared_gate_up_w, L0_ffn_shared_down_w)
    x = x + _L1_xattn_ref(_layernorm(x, axis=-1), ctx_1024, ctx_1024, L1_xattn_W, L1_xattn_b)
    x = x + _L1_ffn_ref(_layernorm(x, axis=-1), L1_ffn_router_w, L1_ffn_w1, L1_ffn_b1, L1_ffn_w2, L1_ffn_b2)
    return x

_drawn_inputs = setup_inputs


def setup_inputs(seed=0):
    import zlib

    import numpy as np

    out = dict(_drawn_inputs(seed))
    spreads = {'L0_xattn_bq': (0.0, 0.292),
     'L0_xattn_bk': (0.0, 0.645),
     'L0_xattn_bv': (0.0, 0.1),
     'L0_xattn_bp': (0.0, 0.1),
     'L0_ffn_ln_gamma': (1.0, 0.2),
     'L0_ffn_ln_beta': (0.0, 0.1),
     'L1_ffn_b1': (0.0, 0.8),
     'L1_ffn_b2': (0.0, 0.545)}
    factors = {'L1_ffn_router_w': 2.755, 'L1_ffn_w1': 3.615, 'L1_ffn_w2': 3.352}
    for name, (base, spread) in spreads.items():
        noise = np.random.default_rng([zlib.crc32(name.encode()), seed]).standard_normal(out[name].shape)
        drawn = base * np.exp(spread * noise) if base else spread * noise
        out[name] = jnp.asarray(drawn.astype(out[name].dtype))
    for name, factor in factors.items():
        out[name] = (out[name] * factor).astype(out[name].dtype)
    return out
```

```python
import math
from collections import namedtuple
from contextlib import ExitStack

import numpy as np

import concourse.bass as bass
from concourse import mybir

NB, TOK, C = 8, 100, 256
KEYS = 361
HEADS = 16
HD = C // HEADS
KC = 2
P = 128
NE = 8
KCH = 3
KR = -(-KEYS // KCH)
KLAST = KEYS - (KCH - 1) * KR
FF0 = 768
FFS = 256
GU = 2 * FF0
FC0 = FF0 // P
EW = KC * GU + FC0 * C
TOPK = 2
TILES = (TOPK * NB * TOK + NE * (P - 1)) // P
SLOTS = TILES * P
FF1 = 1024
FC1 = FF1 // P
CAP = math.ceil(1.5 * NB * TOK / NE)
HALF = CAP // 2
ROWS1 = NE * CAP + NB * TOK
HG = HEADS // KC
KV = P + HG
NT = NB * TOK
HT = NT // 2
SHARED_ORDER = (1, 0)
EPS = 1e-5
BANK = 512

CONST = [("ident", P), ("headmask", KC * KV), ("earlier", P), ("ones", P), ("expert_m", NB * NE),
         ("tile_edge", NE * (TILES // 2)), ("tile_no", TILES), ("cap_base", NB * NE), ("spare_row", NB), ("minus_half", 1), ("eps", 1),
         ("zero", C)]
CONST_AT = {}
_at = 0
for _n, _w in CONST:
    CONST_AT[_n] = (_at, _w)
    _at += _w
CONST_W = _at


def constants():
    c = {n: np.zeros((P, w), np.float32) for n, w in CONST}
    c["ident"][:] = np.eye(P)
    part_head = np.arange(P) // HD
    for g in range(KC):
        c["headmask"][:, g * KV:g * KV + P] = part_head[:, None] == part_head[None, :]
        c["headmask"][:, g * KV + P:(g + 1) * KV] = part_head[:, None] == np.arange(HG)[None, :]
    t = np.arange(P)
    c["earlier"][:] = (t[:, None] < t[None, :]) & (t[None, :] < TOK) & (t[:, None] < TOK)
    c["ones"][:] = 1.0
    c["expert_m"][:] = np.tile(np.arange(NE) - NE, NB)
    c["tile_edge"][:] = np.tile(P * np.arange(TILES // 2), NE)
    c["tile_no"][:] = np.arange(TILES)
    c["cap_base"][:] = np.tile(CAP * np.arange(NE), NB)
    c["spare_row"][:] = NE * CAP + TOK * np.arange(NB)[None, :] + t[:, None]
    c["minus_half"][:] = -0.5
    c["eps"][:] = EPS
    return np.concatenate([c[n] for n, _ in CONST], axis=1)


def after(eng, sem, n):
    if isinstance(n, int) and n <= 0:
        return
    eng.wait_ge(sem, n)


def after_alone(eng, sem, n):
    after(eng, sem, n)
    if not isinstance(n, int):
        eng.nop(nofuse=True)


Beat = namedtuple("Beat", "n half pair")


def beat(j, k):
    return Beat(2 * j + k, k % 2, j + k // 2)


SEMS = """
x_in consts_in attn_w_in ctx_even ctx_odd small_in experts_in zeroed
mv0 rstd0 xn_ready xn_transposed xnT_ready
kq_done kq_biased kq_max kq_centered kq_exp v_done v_copied kq_sum kq_recip q_ready vr_ready
kv_done kvm_ready q_transposed qT_ready attn_done den_recip attn_scaled q_plus_bv o_ready o_transposed oT_ready
proj_done x_plus_bp x1_ready
mv1 rstd1 n1_ready mv2 rstd2 n2_ready scaled_by_gamma nrm_ready nrm_kept nrm_transposed nrmT_ready
st0 st1 st2 ve0 ve1 ve2 zero_pad
logitsT_done logitsT_copied logits_done centred exponentials routing_step gap gap_exp both_hot rank_done rank_copied
tile_off slots_ready scattered
sh_up_done sh_silu sh_hid sh_down_done x1s_ready
xg_even xg_odd xg_transposed xgT_ready gu_done silu_done h_ready h_transposed hT_lo hT_hi down_done y_copied y_even y_odd
yg_even yg_odd wx_in ctx2_even ctx2_odd
comb1 x2_ready st3 mv3 ve3 rstd3 xn3_ready xn3_transposed xn3T_ready
kT_done kT_ready vT_done vn_ready q1_done q1T_ready score_done score_max neg_max p_ready p_recip p_transposed pT_ready
av_done x3_ready st4 mv4 ve4 rstd4 xn4_made xn4_ready xn4_transposed xn4T_ready
r_logitsT_done r_logitsT_copied r_logits_done r_centred r_exponentials r_hots r_rank_done
r_pick r_slots_ready r_scattered
w1_even w1_odd w2_even w2_odd xe_even xe_odd xe_transposed xeT_ready up1_done gelu_done down1_done yT_ready yT_transposed
y1_copied y1_even y1_odd z_even z_odd out_ready out_stored
""".split()
Sems = namedtuple("Sems", SEMS)


def two_layers(nc, x_d, ctx_d, proj_w_d, bias_d, rows_d, routers_d, shared_w_d, experts_d, wx_d, bx_d,
               w1_d, b1_d, w2_d, b2_d, consts_d, out_d):
    f32, u32, i32 = mybir.dt.float32, mybir.dt.uint32, mybir.dt.int32
    ACT, ALU, AX = mybir.ActivationFunctionType, mybir.AluOpType, mybir.AxisListType
    ds = bass.ds
    ctx = ExitStack()
    with ctx:
        def sb(name, cols, dt=f32, rows=P):
            return ctx.enter_context(nc.sbuf_tensor(name, [rows, cols], dt))

        s = Sems(*[ctx.enter_context(nc.semaphore(n)) for n in SEMS])

        xg_dram = nc.dram_tensor("rows_by_slot0", (SLOTS, C), f32, kind="Internal").ap()
        yg_dram = nc.dram_tensor("results_by_slot0", (SLOTS, C), f32, kind="Internal").ap()
        xe_dram = nc.dram_tensor("rows_by_slot1", (ROWS1, C), f32, kind="Internal").ap()
        ye_dram = nc.dram_tensor("results_by_slot1", (NE * CAP, C), f32, kind="Internal").ap()

        wres = sb("wres", NE * EW)
        LATE = 2

        class Region:
            def __init__(self, lo, hi, over=wres):
                self.at, self.hi, self.over = lo, hi, over

            def take(self, cols, rows=P):
                ap = self.over[0:rows, self.at:self.at + cols]
                self.at += cols
                assert self.at <= self.hi
                return ap

        ra = Region((NE - LATE) * EW, NE * EW)
        proj_w = ra.take(4 * KC * C)
        bias4 = ra.take(4 * C)
        rows4 = ra.take(4 * C)
        ctxT = [ra.take(KC * KCH * KR) for _ in range(2)]
        kq = ra.take(4 * C, KR)
        kqe = ra.take(4 * C, KR)
        v_sb = ra.take(KCH * C, KR)
        vr = ra.take(KCH * KC * KV, KR)

        rc = Region(0, NE * EW)
        wx = rc.take(KC * C)
        bx = rc.take(KC)
        ctxT2 = [rc.take(KC * KEYS) for _ in range(2)]
        kT = [rc.take(KC * KEYS) for _ in range(2)]
        v_nat = rc.take(KCH * C, KR)
        q1T = rc.take(KC * TOK)
        xn3 = rc.take(C, TOK)
        xn3T = rc.take(KC * TOK)
        p_sb = rc.take(KCH * KR, TOK)
        pT = rc.take(KCH * TOK, KR)
        yg = [rc.take(TOPK * C, TOK) for _ in range(2)]
        xn4 = rc.take(C, TOK)
        w1 = [rc.take(KC * FF1) for _ in range(2)]
        w2 = [rc.take(FC1 * C) for _ in range(2)]
        xe = [rc.take(2 * C, HALF) for _ in range(2)]
        xeT = rc.take(KC * CAP)
        hidT = rc.take(FC1 * CAP)
        yT = rc.take(KC * CAP)
        y1 = [rc.take(2 * C, HALF) for _ in range(2)]
        z_sb = [rc.take(C, TOK) for _ in range(2)]

        consts = sb("consts", CONST_W)

        def const(name, rows=P):
            at, w = CONST_AT[name]
            return consts[0:rows, at:at + w]

        x_sb = sb("x_sb", NB * C, rows=TOK)
        rows_sb = sb("rows_sb", NB * C, rows=TOK)
        rowsT = sb("rowsT", KC * NT)
        routers = sb("routers", 2 * KC * NE)
        b1 = sb("b1", NE * FC1)
        b2 = sb("b2", NE * KC)
        shared_w = sb("shared_w", KC * 2 * FFS + KC * C)
        sh_hT = sb("sh_hT", KC * NT)
        work = sb("work", 2 * C + KC * P + 3 * FF0 + 2 * C)
        rt = Region(0, work.shape[1], work)
        xg = [rt.take(C) for _ in range(2)]
        xgT = rt.take(KC * P)
        sg = rt.take(FF0)
        h_sb = rt.take(FF0)
        hT = rt.take(FF0)
        y_sb = [rt.take(C) for _ in range(2)]
        logitsT = work[0:NE, 0:NT]
        sh_sg = work[:, NT:NT + KC * HT]
        rs = Region(0, work.shape[1], work)
        xn = rs.take(C, TOK)
        xnT = rs.take(KC * KR)
        q_sb = rs.take(C, TOK)
        q_bv = rs.take(C, TOK)
        qT = rs.take(KC * TOK)
        kvm = rs.take(KC * KV)
        o1 = rs.take(C, TOK)
        o_sb = rs.take(C, TOK)
        oT = rs.take(KC * TOK)
        xbp = rs.take(C, TOK)
        n1 = rs.take(C, TOK)
        n2 = rs.take(C, TOK)
        nrm = rs.take(C, TOK)
        kq_m = sb("kq_m", 4 * HEADS, rows=KR)
        kq_s = sb("kq_s", 4 * HEADS, rows=KR)
        kq_r = sb("kq_r", 4 * HEADS, rows=KR)
        den = sb("den", KC * HG, rows=TOK)
        bn = [sb(f"bn{i}", 6, rows=TOK) for i in range(5)]
        mv = [sb(f"mv{i}", 2, rows=TOK) for i in range(5)]
        ve = [sb(f"ve{i}", 1, rows=TOK) for i in range(5)]
        rstd = [sb(f"rstd{i}", 1, rows=TOK) for i in range(5)]
        p_max = sb("p_max", 1, rows=TOK)
        p_neg = sb("p_neg", 1, rows=TOK)
        p_sum = sb("p_sum", 1, rows=TOK)
        p_rec = sb("p_rec", 1, rows=TOK)
        be = {n: sb("rt_" + n, NB * NE, rows=TOK) for n in "cent exp probs eq eqm hot1 masked hot2 rows pick1 pick2".split()}
        tb = {n: sb("rt_" + n, NB, rows=TOK) for n in "max sum rec idx top1 top2 gap egap gden g1 g2 slot1 slot2 pos base kept raw rel relk w".split()}
        hots = sb("hots", (NB + 1) * NE, rows=TOK)
        rank = sb("rank", (NB + 1) * NE)
        over_edge = sb("over_edge", NE * (TILES // 2))
        tiles_n = sb("tiles_n", NE)
        tiles_scan = sb("tiles_scan", NE)
        first_tile = sb("first_tile", NE)
        base_row = sb("base_row", NE)
        zero8 = sb("zero8", NE)
        tile_cmp = sb("tile_cmp", TILES * NE, rows=1)
        tile_expert = sb("tile_expert", TILES, rows=1)
        tile_off = sb("tile_off", TILES, i32, rows=1)
        slots0 = sb("slots0", TOPK * NB, u32, rows=TOK)
        slots1 = sb("slots1", 2 * NB, u32, rows=TOK)

        psum = ctx.enter_context(nc.psum_tensor("psum", [P, 8 * BANK], f32))

        def bank(n, cols=BANK, rows=P, at=0):
            return psum[0:rows, n * BANK + at:n * BANK + at + cols]

        ident = const("ident")

        def split(ap, n):
            return ap.rearrange("p (n m) -> p n m", n=n)

        def each(ap, m):
            return ap.unsqueeze(2).to_broadcast([ap.shape[0], ap.shape[1], m])

        def row(t, n, w=C):
            return t[:, ds(n * w, w)]

        def ctx_half(b):
            return (s.ctx_even, s.ctx_odd)[b.half]

        block = ctx.enter_context(nc.Block())

        @block.sync
        def _(sp):
            sp.dma_start(x_sb[:, :], x_d).then_inc(s.x_in, 16)
            sp.dma_start(consts[:, :], consts_d).then_inc(s.consts_in, 16)

            def load_ctx(b):
                sp.dma_start(split(ctxT[b.half], KC)[:, :, 0:KEYS],
                             ctx_d[ds(b.n, 1)].rearrange("b p (k n) -> (b p) k n", k=KC)).then_inc(ctx_half(b), 16)

            load_ctx(beat(0, 0))
            sp.dma_start(proj_w, proj_w_d).then_inc(s.attn_w_in, 16)
            sp.dma_start(bias4, bias_d).then_inc(s.attn_w_in, 16)
            load_ctx(beat(0, 1))
            sp.dma_start(rows4, rows_d).then_inc(s.attn_w_in, 16)

            def load_expert(n):
                sp.dma_start(wres[:, ds(n * EW, EW)], experts_d[ds(n, 1)].rearrange("e p n -> (e p) n")).then_inc(s.experts_in, 16)

            with sp.Fori(0, NB // 2 - 1, 1) as j:
                for k in range(2):
                    b = beat(j, k)
                    load_expert(b.n)
                    after(sp, s.v_done, b.n + 1)
                    load_ctx(beat(j, k + 2))
            sp.dma_start(shared_w[:, :], shared_w_d).then_inc(s.small_in, 16)
            sp.dma_start(routers[:, :], routers_d).then_inc(s.small_in, 16)
            sp.dma_start(b1[:, :], b1_d).then_inc(s.small_in, 16)
            sp.dma_start(b2[:, :], b2_d).then_inc(s.small_in, 16)
            after(sp, s.proj_done, NB)
            after(sp, s.nrm_ready, NB)
            for n in range(NE - LATE, NE):
                load_expert(n)

            def load_rows0(i):
                half = (s.xg_even, s.xg_odd)[i.half]
                sp.dma_start(xg[i.half], xg_dram[ds(i.n * P, P), :]).then_inc(half, 16)

            after(sp, s.scattered, 16 * TOPK * NB)
            load_rows0(beat(0, 0))
            load_rows0(beat(0, 1))
            with sp.Fori(0, TILES // 2 - 1, 1) as j:
                for k in range(2):
                    i = beat(j, k)
                    after(sp, s.xg_transposed, i.n + 1)
                    load_rows0(beat(j, k + 2))

            after(sp, s.down_done, TILES)
            sp.dma_start(wx, wx_d).then_inc(s.wx_in, 16)
            sp.dma_start(bx, bx_d).then_inc(s.wx_in, 16)

            def load_ctx2(b):
                sp.dma_start(split(ctxT2[b.half], KC), ctx_d[ds(b.n, 1)].rearrange("b p (k n) -> (b p) k n", k=KC)).then_inc((s.ctx2_even, s.ctx2_odd)[b.half], 16)

            load_ctx2(beat(0, 0))
            load_ctx2(beat(0, 1))

            def load_w1(e):
                sp.dma_start(w1[e.half], w1_d[ds(e.n, 1)].rearrange("e p n -> (e p) n")).then_inc((s.w1_even, s.w1_odd)[e.half], 16)

            def load_w2(e):
                sp.dma_start(w2[e.half], w2_d[ds(e.n, 1)].rearrange("e p n -> (e p) n")).then_inc((s.w2_even, s.w2_odd)[e.half], 16)

            for k in range(2):
                load_w1(beat(0, k))
                load_w2(beat(0, k))
            with sp.Fori(0, NB // 2 - 1, 1) as j:
                for k in range(2):
                    after(sp, s.kT_done, beat(j, k).n + 1)
                    load_ctx2(beat(j, k + 2))

            def load_rows1(e):
                sp.dma_start(split(xe[e.half], 2), xe_dram[ds(e.n * CAP, CAP), :].rearrange("(m p) c -> p m c", p=HALF)).then_inc((s.xe_even, s.xe_odd)[e.half], 16)

            after(sp, s.r_scattered, 16 * NB)
            load_rows1(beat(0, 0))
            load_rows1(beat(0, 1))
            with sp.Fori(0, NE // 2 - 1, 1) as j:
                for k in range(2):
                    e = beat(j, k)
                    after(sp, s.xe_transposed, e.n + 1)
                    load_rows1(beat(j, k + 2))
                    after(sp, s.up1_done, FC1 * (e.n + 1))
                    load_w1(beat(j, k + 2))
                    after(sp, s.down1_done, e.n + 1)
                    load_w2(beat(j, k + 2))
            for n in range(NB):
                after(sp, s.out_ready, n + 1)
                sp.dma_start(out_d[n, :, :], row(x_sb, n)).then_inc(s.out_stored, 16)
            sp.wait_ge(s.out_stored, 16 * NB)

        @block.gpsimd
        def _(pool):
            def tt(out, a, b, op):
                return nc.gpsimd.tensor_tensor(out, a, b, op)

            after(pool, s.consts_in, 16)
            zeros = const("zero")
            pool.dma_start(xg_dram.rearrange("(p s) c -> p s c", p=P),
                           zeros.unsqueeze(1).to_broadcast([P, SLOTS // P, C])).then_inc(s.zeroed, 16)
            pool.dma_start(xe_dram[0:NE * CAP, :].rearrange("(p s) c -> p s c", p=NE * CAP // 10),
                           zeros[0:NE * CAP // 10, :].unsqueeze(1).to_broadcast([NE * CAP // 10, 10, C])).then_inc(s.zeroed, 16)

            def inverse_deviation(kind, b, mv_sem, ve_sem, rstd_sem):
                after(pool, mv_sem, b.n + 1)
                tt(ve[kind][:, :], mv[kind][:, 1:2], const("eps", TOK), ALU.add).then_inc(ve_sem, 1)
                pool.wait_ge(ve_sem, b.n + 1)
                tt(rstd[kind][:, :], ve[kind][:, :], const("minus_half", TOK), ALU.pow).then_inc(rstd_sem, 1)

            def beat_a(a, b, c, nxt):
                if nxt:
                    inverse_deviation(0, nxt, s.mv0, s.ve0, s.rstd0)
                if c:
                    tt(xbp, row(x_sb, c.n), rows4[0:TOK, C:2 * C], ALU.add).then_inc(s.x_plus_bp, 1)
                    inverse_deviation(1, c, s.mv1, s.ve1, s.rstd1)
                if a:
                    after(pool, s.kq_max, a.n + 1)
                    tt(split(kq, 4 * HEADS), split(kq, 4 * HEADS), each(kq_m[:, :], HD), ALU.subtract).then_inc(s.kq_centered, 1)
                if c:
                    inverse_deviation(2, c, s.mv2, s.ve2, s.rstd2)
                    after(pool, s.n2_ready, c.n + 1)
                    tt(n2, n2, rows4[0:TOK, 2 * C:3 * C], ALU.mult).then_inc(s.scaled_by_gamma, 1)
                    if not a:
                        after(pool, s.nrm_transposed, c.n)
                    pool.wait_ge(s.scaled_by_gamma, c.n + 1)
                    tt(nrm, n2, rows4[0:TOK, 3 * C:4 * C], ALU.add).then_inc(s.nrm_ready, 1)
                    pool.wait_ge(s.nrm_ready, c.n + 1)
                    nc.gpsimd.tensor_copy(row(rows_sb, c.n), nrm).then_inc(s.nrm_kept, 1)
                if a:
                    after(pool, s.kq_recip, a.n + 1)
                    after(pool, s.q_transposed, a.n)
                    after(pool, s.q_plus_bv, a.n)
                    tt(split(q_sb, HEADS), split(kqe[0:TOK, 3 * C:4 * C], HEADS),
                       each(kq_r[0:TOK, 3 * HEADS:4 * HEADS], HD), ALU.mult).then_inc(s.q_ready, 1)
                    after(pool, s.o_ready, a.n)
                    pool.wait_ge(s.q_ready, a.n + 1)
                    tt(q_bv, q_sb, rows4[0:TOK, 0:C], ALU.add).then_inc(s.q_plus_bv, 1)

            inverse_deviation(0, beat(0, 0), s.mv0, s.ve0, s.rstd0)
            after(pool, s.attn_w_in, 48)
            beat_a(beat(0, 0), None, None, beat(0, 1))
            beat_a(beat(0, 1), beat(0, 0), None, beat(0, 2))
            with pool.Fori(0, NB // 2 - 2, 1) as j:
                for k in range(2):
                    beat_a(beat(j, k + 2), beat(j, k + 1), beat(j, k), beat(j, k + 3))
            for k in range(NB - 2, NB + 2):
                beat_a(beat(0, k) if k < NB else None, beat(0, k - 1) if k - 1 < NB else None, beat(0, k - 2),
                       beat(0, k + 1) if k + 1 < NB else None)

            pool.wait_ge(s.zeroed, 32)
            pool.wait_ge(s.nrm_kept, NB)
            pool.wait_ge(s.slots_ready, 2)
            for n in range(NB):
                for k in range(TOPK):
                    nc.gpsimd.indirect_dma_start(
                        out=xg_dram, out_offset=bass.IndirectOffsetOnAxis(ap=slots0[:, k * NB + n:k * NB + n + 1], axis=0),
                        in_=rows_sb[:, n * C:(n + 1) * C], in_offset=None).then_inc(s.scattered, 16)

            after(pool, s.y_even, 16 * (TILES // 2 + 1))
            after(pool, s.y_odd, 16 * (TILES // 2 + 1))
            after(pool, s.down_done, TILES)
            for n in range(NB):
                b = beat(0, n)
                after(pool, s.x2_ready, n - 1)
                for k in range(TOPK):
                    nc.gpsimd.indirect_dma_start(
                        out=yg[b.half][:, k * C:(k + 1) * C], out_offset=None, in_=yg_dram,
                        in_offset=bass.IndirectOffsetOnAxis(ap=slots0[:, k * NB + n:k * NB + n + 1], axis=0)
                    ).then_inc((s.yg_even, s.yg_odd)[b.half], 16)
                inverse_deviation(3, b, s.mv3, s.ve3, s.rstd3)
                if n:
                    inverse_deviation(4, beat(0, n - 1), s.mv4, s.ve4, s.rstd4)
            inverse_deviation(4, beat(0, NB - 1), s.mv4, s.ve4, s.rstd4)

            pool.wait_ge(s.zeroed, 32)
            pool.wait_ge(s.xn4_ready, NB)
            pool.wait_ge(s.r_slots_ready, 2)
            for n in range(NB):
                nc.gpsimd.indirect_dma_start(
                    out=xe_dram, out_offset=bass.IndirectOffsetOnAxis(ap=slots1[:, n:n + 1], axis=0),
                    in_=rows_sb[:, n * C:(n + 1) * C], in_offset=None).then_inc(s.r_scattered, 16)
            after(pool, s.y1_even, 16 * (NE // 2 + 1))
            after(pool, s.y1_odd, 16 * (NE // 2 + 1))
            for n in range(NB):
                b = beat(0, n)
                after(pool, s.out_ready, n - 1)
                nc.gpsimd.indirect_dma_start(
                    out=z_sb[b.half], out_offset=None, in_=ye_dram,
                    in_offset=bass.IndirectOffsetOnAxis(ap=slots1[:, NB + n:NB + n + 1], axis=0)
                ).then_inc((s.z_even, s.z_odd)[b.half], 16)

        @block.scalar
        def _(act):
            def copy(out, in_):
                return nc.scalar.copy(out, in_)

            for counted in (s.nrmT_ready, s.xn4T_ready):
                act.sem_inc(counted, 1)
            for counted in (s.y_even, s.y_odd, s.y1_even, s.y1_odd):
                act.sem_inc(counted, 16)

            def beat_a(a, b, c):
                if a:
                    after(act, s.xn_transposed, a.n + 1)
                    after(act, s.kq_done, a.n)
                    copy(split(xnT, KC)[:, :, 0:TOK], split(bank(4, KC * TOK), KC)).then_inc(s.xnT_ready, 1)
                if c:
                    after(act, s.o_transposed, c.n + 1)
                    copy(oT, bank(5, KC * TOK)).then_inc(s.oT_ready, 1)
                if a:
                    after(act, s.v_done, a.n + 1)
                    after(act, s.vr_ready, a.n)
                    copy(v_sb, bank(2, KCH * C, KR)).then_inc(s.v_copied, 1)
                    after(act, s.kq_centered, a.n + 1)
                    after(act, s.kv_done, a.n)
                    after(act, s.q_ready, a.n)
                    after(act, s.kq_sum, a.n)
                    nc.scalar.activation(kqe, kq, ACT.Exp).then_inc(s.kq_exp, 1)
                if b:
                    after(act, s.q_transposed, b.n + 1)
                    after(act, s.attn_done, b.n)
                    copy(qT, bank(5, KC * TOK)).then_inc(s.qT_ready, 1)
                if c:
                    after(act, s.nrm_transposed, c.n + 1)
                    copy(split(rowsT[:, :], KC)[:, :, ds(c.n * TOK, TOK)], split(bank(4, KC * TOK), KC)).then_inc(s.nrmT_ready, 1)

            beat_a(beat(0, 0), None, None)
            beat_a(beat(0, 1), beat(0, 0), None)
            with act.Fori(0, NB // 2 - 1, 1) as j:
                for k in range(2):
                    beat_a(beat(j, k + 2), beat(j, k + 1), beat(j, k))
            beat_a(None, beat(0, NB - 1), beat(0, NB - 2))
            beat_a(None, None, beat(0, NB - 1))

            for h in range(2):
                after(act, s.logitsT_done, h + 1)
                copy(logitsT[:, h * HT:(h + 1) * HT], bank(h, HT, NE)).then_inc(s.logitsT_copied, 1)
            act.wait_ge(s.centred, 1)
            nc.scalar.activation(be["exp"][:, :], be["cent"][:, :], ACT.Exp).then_inc(s.exponentials, 1)
            act.wait_ge(s.gap, 1)
            nc.scalar.activation(tb["egap"][:, :], tb["gap"][:, :], ACT.Exp).then_inc(s.gap_exp, 1)
            act.wait_ge(s.nrm_kept, NB)
            for m, h in enumerate(SHARED_ORDER):
                for g in range(KC):
                    after(act, s.sh_up_done, KC * m + g + 1)
                    after(act, s.sh_hid, KC * (m - 1) + g + 1)
                    nc.scalar.activation(sh_sg[:, g * HT:(g + 1) * HT], bank(4 * h + 2 * g, HT), ACT.Silu).then_inc(s.sh_silu, 1)

            def tile(i, last):
                for j3 in range(3):
                    after(act, s.gu_done, 3 * i.n + j3 + 1)
                    after(act, s.h_ready, 3 * i.n + j3 - 2)
                    nc.scalar.activation(sg[:, j3 * C:(j3 + 1) * C], bank(j3, C), ACT.Silu).then_inc(s.silu_done, 1)
                if last:
                    result(last)
                after(act, s.h_transposed, 2 * i.n + 2)
                after(act, s.down_done, i.n)
                copy(hT[:, FF0 // 2:], bank(4, FF0 // 2)).then_inc(s.hT_hi, 1)

            def result(i):
                stored = (s.y_even, s.y_odd)[i.half]
                after(act, s.down_done, i.n + 1)
                after(act, stored, 16 * (i.pair + 1))
                copy(y_sb[i.half], bank(5, C)).then_inc(s.y_copied, 1)
                act.wait_ge(s.y_copied, i.n + 1)
                act.dma_start(yg_dram[ds(i.n * P, P), :], y_sb[i.half]).then_inc(stored, 16)

            tile(beat(0, 0), None)
            with act.Fori(0, TILES // 2 - 1, 1) as j:
                for k in range(1, 3):
                    tile(beat(j, k), beat(j, k - 1))
            tile(beat(0, TILES - 1), beat(0, TILES - 2))
            result(beat(0, TILES - 1))

            act.wait_ge(s.wx_in, 32)

            def beat_c(a, b, c):
                if b:
                    after(act, s.xn3_transposed, b.n + 1)
                    after(act, s.q1_done, b.n)
                    copy(xn3T, bank(4, KC * TOK)).then_inc(s.xn3T_ready, 1)
                    after(act, s.q1_done, b.n + 1)
                    after(act, s.score_done, b.n)
                    for g in range(KC):
                        nc.scalar.activation(q1T[:, g * TOK:(g + 1) * TOK], bank(5, TOK, at=g * TOK), ACT.Identity,
                                             bias=bx[:, g:g + 1]).then_inc(s.q1T_ready, 1)
                if a:
                    after(act, s.kT_done, a.n + 1)
                    after(act, s.score_done, a.n - 1)
                    after(act, s.vT_done, a.n - 1)
                    for g in range(KC):
                        nc.scalar.activation(kT[a.half][:, g * KEYS:(g + 1) * KEYS], bank(g, KEYS), ACT.Identity,
                                             bias=bx[:, g:g + 1]).then_inc(s.kT_ready, 1)
                if b:
                    after(act, s.neg_max, b.n + 1)
                    after(act, s.p_transposed, b.n)
                    nc.scalar.activation(p_sb[:, 0:KEYS], bank(6, KEYS, TOK), ACT.Exp, bias=p_neg[:, :], scale=1.0 / math.sqrt(C),
                                         accum_out=p_sum[:, :]).then_inc(s.p_ready, 1)
                    after(act, s.p_transposed, b.n + 1)
                    after(act, s.av_done, b.n)
                    full = (KCH - 1) * TOK
                    copy(pT[:, 0:full], bank(5, full, KR))
                    copy(pT[0:KLAST, full:], bank(5, TOK, KLAST, at=full)).then_inc(s.pT_ready, 1)
                if c:
                    after(act, s.xn4_transposed, c.n + 1)
                    copy(split(rowsT[:, :], KC)[:, :, ds(c.n * TOK, TOK)], split(bank(4, KC * TOK), KC)).then_inc(s.xn4T_ready, 1)

            beat_c(beat(0, 0), None, None)
            beat_c(beat(0, 1), beat(0, 0), None)
            with act.Fori(0, NB // 2 - 1, 1) as j:
                for k in range(2):
                    beat_c(beat(j, k + 2), beat(j, k + 1), beat(j, k))
            beat_c(None, beat(0, NB - 1), beat(0, NB - 2))
            beat_c(None, None, beat(0, NB - 1))

            for h in range(2):
                after(act, s.r_logitsT_done, h + 1)
                copy(logitsT[:, h * HT:(h + 1) * HT], bank(h, HT, NE)).then_inc(s.r_logitsT_copied, 1)
            act.wait_ge(s.r_centred, 1)
            nc.scalar.activation(be["exp"][:, :], be["cent"][:, :], ACT.Exp).then_inc(s.r_exponentials, 1)
            act.wait_ge(s.small_in, 16 * 4)

            def expert(e, last):
                for j8 in range(FC1):
                    after(act, s.up1_done, FC1 * e.n + j8 + 1)
                    after(act, s.down1_done, e.n)
                    nc.scalar.activation(hidT[:, j8 * CAP:(j8 + 1) * CAP], bank(j8 % 3, CAP), ACT.Gelu,
                                         bias=b1[:, ds(e.n * FC1 + j8, 1)]).then_inc(s.gelu_done, 1)
                if last:
                    result1(last)

            def result1(e):
                stored = (s.y1_even, s.y1_odd)[e.half]
                after(act, s.yT_transposed, e.n + 1)
                after(act, stored, 16 * (e.pair + 1))
                copy(y1[e.half], bank(6, 2 * C, HALF)).then_inc(s.y1_copied, 1)
                act.wait_ge(s.y1_copied, e.n + 1)
                act.dma_start(ye_dram[ds(e.n * CAP, CAP), :].rearrange("(m p) c -> p m c", p=HALF),
                              split(y1[e.half], 2)).then_inc(stored, 16)

            expert(beat(0, 0), None)
            with act.Fori(0, NE // 2 - 1, 1) as j:
                for k in range(1, 3):
                    expert(beat(j, k), beat(j, k - 1))
            expert(beat(0, NE - 1), beat(0, NE - 2))
            result1(beat(0, NE - 1))

        @block.vector
        def _(dve):
            def tt(out, a, b, op):
                return nc.vector.tensor_tensor(out, a, b, op)

            def reduce(out, in_, op):
                return nc.vector.tensor_reduce(out, in_, AX.X, op)

            def moments(kind, b, src, st_sem, mv_sem):
                nc.vector.bn_stats(bn[kind][:, :], src).then_inc(st_sem, 1)
                after_alone(dve, st_sem, b.n + 1)
                nc.vector.bn_aggr(mv[kind][:, :], bn[kind][:, :]).then_inc(mv_sem, 1)

            def normalise(kind, b, out, src, mv_sem, rstd_sem):
                dve.wait_ge(mv_sem, b.n + 1)
                after(dve, rstd_sem, b.n + 1)
                return nc.vector.tensor_scalar(out, src, mv[kind][:, 0:1], rstd[kind][:, :], ALU.subtract, ALU.mult)

            def first_norm_moments(b):
                moments(0, b, row(x_sb, b.n), s.st0, s.mv0)

            def first_norm(b):
                after(dve, s.xn_transposed, b.n)
                normalise(0, b, xn, row(x_sb, b.n), s.mv0, s.rstd0).then_inc(s.xn_ready, 1)

            for t in ctxT:
                nc.vector.memset(split(t, KC)[:, :, KEYS:KCH * KR], 0.0).then_inc(s.zero_pad, 1)
            nc.vector.memset(split(xnT, KC)[:, :, TOK:KR], 0.0).then_inc(s.zero_pad, 1)
            nc.vector.memset(hots[:, NB * NE:], 0.0).then_inc(s.zero_pad, 1)
            nc.vector.memset(zero8[:, :], 0.0).then_inc(s.zero_pad, 1)
            after(dve, s.x_in, 16)
            first_norm_moments(beat(0, 0))
            first_norm(beat(0, 0))
            after(dve, s.attn_w_in, 48)
            after(dve, s.consts_in, 16)

            def beat_a(a, b, c, nxt):
                if c:
                    after(dve, s.attn_done, c.n + 1)
                    num = split(bank(7, KC * KV, TOK), KC)
                    nc.vector.reciprocal(split(den[:, :], KC), num[:, :, P:KV]).then_inc(s.den_recip, 1)
                    dve.wait_ge(s.den_recip, c.n + 1)
                    for g in range(KC):
                        tt(split(o1[:, g * P:(g + 1) * P], HG), split(num[:, g, 0:P], HG),
                           each(den[:, g * HG:(g + 1) * HG], HD), ALU.mult).then_inc(s.attn_scaled, 1)
                    after(dve, s.q_plus_bv, c.n + 1)
                    dve.wait_ge(s.attn_scaled, KC * (c.n + 1))
                    tt(o_sb, o1, q_bv, ALU.add).then_inc(s.o_ready, 1)
                if nxt:
                    first_norm_moments(nxt)
                if a:
                    after(dve, s.kq_done, a.n + 1)
                    after(dve, s.kq_exp, a.n)
                    tt(kq, bank(0, 4 * C, KR), bias4[0:KR, :], ALU.add).then_inc(s.kq_biased, 1)
                if nxt:
                    first_norm(nxt)
                if a:
                    dve.wait_ge(s.kq_biased, a.n + 1)
                    reduce(kq_m[:, :], split(kq, 4 * HEADS), ALU.max).then_inc(s.kq_max, 1)
                if c:
                    after(dve, s.proj_done, c.n + 1)
                    after(dve, s.x_plus_bp, c.n + 1)
                    tt(row(x_sb, c.n), bank(6, C, TOK), xbp, ALU.add).then_inc(s.x1_ready, 1)
                    after_alone(dve, s.x1_ready, c.n + 1)
                    moments(1, c, row(x_sb, c.n), s.st1, s.mv1)
                    normalise(1, c, n1, row(x_sb, c.n), s.mv1, s.rstd1).then_inc(s.n1_ready, 1)
                    dve.wait_ge(s.n1_ready, c.n + 1)
                    moments(2, c, n1, s.st2, s.mv2)
                if b:
                    after(dve, s.kv_done, b.n + 1)
                    after(dve, s.attn_done, b.n)
                    tt(kvm, bank(6, KC * KV), const("headmask"), ALU.mult).then_inc(s.kvm_ready, 1)
                if c:
                    normalise(2, c, n2, n1, s.mv2, s.rstd2).then_inc(s.n2_ready, 1)
                if a:
                    after(dve, s.kq_exp, a.n + 1)
                    reduce(kq_s[:, :], split(kqe, 4 * HEADS), ALU.add).then_inc(s.kq_sum, 1)
                    dve.wait_ge(s.kq_sum, a.n + 1)
                    after(dve, s.q_ready, a.n)
                    nc.vector.reciprocal(kq_r[:, :], kq_s[:, :]).then_inc(s.kq_recip, 1)
                    dve.wait_ge(s.kq_recip, a.n + 1)
                    after(dve, s.v_copied, a.n + 1)
                    after(dve, s.kv_done, a.n)
                    vr_v = vr.rearrange("p (c g n) -> p c g n", c=KCH, g=KC)
                    for g in range(KC):
                        per_head = split(kq_r[:, 0:KCH * HEADS], KCH)[:, :, g * HG:(g + 1) * HG]
                        tt(vr_v[:, :, g, 0:P].rearrange("p c (h d) -> p c h d", h=HG),
                           split(v_sb, KCH)[:, :, g * P:(g + 1) * P].rearrange("p c (h d) -> p c h d", h=HG),
                           per_head.unsqueeze(3).to_broadcast([KR, KCH, HG, HD]), ALU.mult)
                        last = nc.vector.tensor_copy(vr_v[:, :, g, P:KV], per_head)
                    last.then_inc(s.vr_ready, 1)

            beat_a(beat(0, 0), None, None, beat(0, 1))
            beat_a(beat(0, 1), beat(0, 0), None, beat(0, 2))
            with dve.Fori(0, NB // 2 - 2, 1) as j:
                for k in range(2):
                    beat_a(beat(j, k + 2), beat(j, k + 1), beat(j, k), beat(j, k + 3))
            for k in range(NB - 2, NB + 2):
                beat_a(beat(0, k) if k < NB else None, beat(0, k - 1) if k - 1 < NB else None, beat(0, k - 2),
                       beat(0, k + 1) if k + 1 < NB else None)

            steps = [0]

            def then(ins):
                steps[0] += 1
                ins.then_inc(s.routing_step, 1)
                dve.wait_ge(s.routing_step, steps[0])

            def by_token(n):
                return split(be[n][:, :], NB)

            def probabilities(logits_sem, centred, exponentials):
                after(dve, logits_sem, 1)
                logits = split(bank(2, NB * NE, TOK), NB)
                then(reduce(tb["max"][:, :], logits, ALU.max))
                tt(by_token("cent"), logits, each(tb["max"][:, :], NE), ALU.subtract).then_inc(centred, 1)
                after(dve, exponentials, 1)
                then(reduce(tb["sum"][:, :], by_token("exp"), ALU.add))
                then(nc.vector.reciprocal(tb["rec"][:, :], tb["sum"][:, :]))
                then(tt(by_token("probs"), by_token("exp"), each(tb["rec"][:, :], NE), ALU.mult))

            expert_m = split(const("expert_m", TOK), NB)

            def first_largest(src, top, hot):
                then(reduce(tb[top][:, :], by_token(src), ALU.max))
                then(tt(by_token("eq"), by_token(src), each(tb[top][:, :], NE), ALU.is_equal))
                then(tt(by_token("eqm"), by_token("eq"), expert_m, ALU.mult))
                then(reduce(tb["idx"][:, :], by_token("eqm"), ALU.min))
                then(tt(by_token(hot), expert_m, each(tb["idx"][:, :], NE), ALU.is_equal))

            probabilities(s.logits_done, s.centred, s.exponentials)
            first_largest("probs", "top1", "hot1")
            then(nc.vector.scalar_tensor_tensor(be["masked"][:, :], be["hot1"][:, :], -4.0, be["probs"][:, :], ALU.mult, ALU.add))
            first_largest("masked", "top2", "hot2")
            tt(hots[:, 0:NB * NE], be["hot1"][:, :], be["hot2"][:, :], ALU.add).then_inc(s.both_hot, 1)
            tt(tb["gap"][:, :], tb["top2"][:, :], tb["top1"][:, :], ALU.subtract).then_inc(s.gap, 1)
            after(dve, s.gap_exp, 1)
            then(nc.vector.tensor_scalar(tb["gden"][:, :], tb["egap"][:, :], 1.0, None, ALU.add))
            then(nc.vector.reciprocal(tb["g1"][:, :], tb["gden"][:, :]))
            then(tt(tb["g2"][:, :], tb["egap"][:, :], tb["g1"][:, :], ALU.mult))
            after(dve, s.rank_done, 1)
            nc.vector.tensor_copy(rank[:, :], bank(3, (NB + 1) * NE)).then_inc(s.rank_copied, 1)
            dve.wait_ge(s.rank_copied, 1)
            then(tt(split(over_edge[:, :], NE), each(rank[:, NB * NE:], TILES // 2), split(const("tile_edge"), NE), ALU.is_gt))
            then(reduce(tiles_n[:, :], split(over_edge[:, :], NE), ALU.add))
            then(nc.vector.tensor_tensor_scan(tiles_scan[:, :], tiles_n[:, :], zero8[:, :], 0.0, ALU.add, ALU.add))
            then(tt(first_tile[:, :], tiles_scan[:, :], tiles_n[:, :], ALU.subtract))
            then(nc.vector.tensor_scalar(base_row[:, :], first_tile[:, :], float(P), None, ALU.mult))
            then(tt(by_token("rows"), split(rank[0:TOK, 0:NB * NE], NB),
                    base_row[0:TOK, :].unsqueeze(1).to_broadcast([TOK, NB, NE]), ALU.add))
            for k, (hot, pick, slot) in enumerate((("hot1", "pick1", "slot1"), ("hot2", "pick2", "slot2"))):
                then(tt(be[pick][:, :], be["rows"][:, :], be[hot][:, :], ALU.mult))
                then(reduce(tb[slot][:, :], by_token(pick), ALU.add))
                nc.vector.tensor_copy(slots0[:, k * NB:(k + 1) * NB], tb[slot][:, :]).then_inc(s.slots_ready, 1)
            then(tt(split(tile_cmp[:, :], TILES), each(const("tile_no", 1), NE),
                    tiles_scan[0:1, :].unsqueeze(1).to_broadcast([1, TILES, NE]), ALU.is_ge))
            then(reduce(tile_expert[:, :], split(tile_cmp[:, :], TILES), ALU.add))
            nc.vector.tensor_scalar(tile_off[:, :], tile_expert[:, :], float(NE - 1), float(EW), ALU.min, ALU.mult).then_inc(s.tile_off, 1)

            for m, h in enumerate(SHARED_ORDER):
                for g in range(KC):
                    after(dve, s.sh_silu, KC * m + g + 1)
                    tt(sh_hT[:, g * NT + h * HT:g * NT + (h + 1) * HT], sh_sg[:, g * HT:(g + 1) * HT],
                       bank(4 * h + 2 * g + 1, HT), ALU.mult).then_inc(s.sh_hid, 1)
            for n in range(NB):
                after(dve, s.sh_down_done, n + 1)
                tt(row(x_sb, n), bank(n % 4, C, TOK), row(x_sb, n), ALU.add).then_inc(s.x1s_ready, 1)

            def next_rows(i):
                after(dve, s.xg_transposed, i.n + 1)
                after(dve, s.gu_done, 3 * i.n)
                nc.vector.tensor_copy(xgT, bank(6, KC * P)).then_inc(s.xgT_ready, 1)

            def tile(i, nxt):
                after(dve, s.h_transposed, 2 * i.n)
                for j3 in range(3):
                    after(dve, s.silu_done, 3 * i.n + j3 + 1)
                    tt(h_sb[:, j3 * C:(j3 + 1) * C], sg[:, j3 * C:(j3 + 1) * C], bank(j3, C, at=C), ALU.mult).then_inc(s.h_ready, 1)
                after(dve, s.h_transposed, 2 * i.n + 1)
                after(dve, s.down_done, i.n)
                nc.vector.tensor_copy(hT[:, 0:FF0 // 2], bank(3, FF0 // 2)).then_inc(s.hT_lo, 1)
                if nxt:
                    next_rows(nxt)

            next_rows(beat(0, 0))
            tile(beat(0, 0), beat(0, 1))
            with dve.Fori(0, TILES // 2 - 1, 1) as j:
                for k in range(1, 3):
                    tile(beat(j, k), beat(j, k + 1))
            tile(beat(0, TILES - 1), None)

            def beat_c(a, b, c, nxt):
                if b:
                    after(dve, s.score_done, b.n + 1)
                    reduce(p_max[:, :], bank(6, KEYS, TOK), ALU.max).then_inc(s.score_max, 1)
                    dve.wait_ge(s.score_max, b.n + 1)
                    nc.vector.tensor_scalar(p_neg[:, :], p_max[:, :], -1.0 / math.sqrt(C), None, ALU.mult).then_inc(s.neg_max, 1)
                if nxt:
                    gathered = (s.yg_even, s.yg_odd)[nxt.half]
                    after(dve, gathered, 32 * (nxt.pair + 1))
                    after(dve, s.x1s_ready, NB)
                    y = yg[nxt.half]
                    nc.vector.scalar_tensor_tensor(row(x_sb, nxt.n), y[:, 0:C], tb["g1"][:, ds(nxt.n, 1)], row(x_sb, nxt.n),
                                                   ALU.mult, ALU.add).then_inc(s.comb1, 1)
                    dve.wait_ge(s.comb1, nxt.n + 1)
                    nc.vector.scalar_tensor_tensor(row(x_sb, nxt.n), y[:, C:2 * C], tb["g2"][:, ds(nxt.n, 1)], row(x_sb, nxt.n),
                                                   ALU.mult, ALU.add).then_inc(s.x2_ready, 1)
                    after_alone(dve, s.x2_ready, nxt.n + 1)
                    moments(3, nxt, row(x_sb, nxt.n), s.st3, s.mv3)
                if a:
                    after(dve, s.vT_done, a.n + 1)
                    after(dve, s.av_done, a.n)
                    full = (KCH - 1) * C
                    nc.vector.tensor_copy(v_nat[:, 0:full], bank(2, full, KR))
                    nc.vector.tensor_copy(v_nat[0:KLAST, full:], bank(2, C, KLAST, at=full)).then_inc(s.vn_ready, 1)
                if nxt:
                    after(dve, s.xn3_transposed, nxt.n)
                    normalise(3, nxt, xn3, row(x_sb, nxt.n), s.mv3, s.rstd3).then_inc(s.xn3_ready, 1)
                if b:
                    after(dve, s.p_ready, b.n + 1)
                    nc.vector.reciprocal(p_rec[:, :], p_sum[:, :]).then_inc(s.p_recip, 1)
                    dve.wait_ge(s.p_recip, b.n + 1)
                    after(dve, s.av_done, b.n + 1)
                    nc.vector.scalar_tensor_tensor(row(x_sb, b.n), bank(7, C, TOK), p_rec[:, :], row(x_sb, b.n),
                                                   ALU.mult, ALU.add).then_inc(s.x3_ready, 1)
                    after_alone(dve, s.x3_ready, b.n + 1)
                    moments(4, b, row(x_sb, b.n), s.st4, s.mv4)
                    after(dve, s.xn4_transposed, b.n)
                    normalise(4, b, xn4, row(x_sb, b.n), s.mv4, s.rstd4).then_inc(s.xn4_made, 1)
                    dve.wait_ge(s.xn4_made, b.n + 1)
                    nc.vector.tensor_copy(row(rows_sb, b.n), xn4).then_inc(s.xn4_ready, 1)

            beat_c(beat(0, 0), None, None, beat(0, 0))
            beat_c(beat(0, 1), beat(0, 0), None, beat(0, 1))
            with dve.Fori(0, NB // 2 - 1, 1) as j:
                for k in range(2):
                    beat_c(beat(j, k + 2), beat(j, k + 1), beat(j, k), beat(j, k + 2))
            beat_c(None, beat(0, NB - 1), beat(0, NB - 2), None)

            probabilities(s.r_logits_done, s.r_centred, s.r_exponentials)
            first_largest("probs", "top1", "hot1")
            nc.vector.tensor_copy(hots[:, 0:NB * NE], be["hot1"][:, :]).then_inc(s.r_hots, 1)
            then(tt(be["pick2"][:, :], be["hot1"][:, :], const("cap_base", TOK), ALU.mult))
            then(reduce(tb["base"][:, :], by_token("pick2"), ALU.add))
            after(dve, s.r_rank_done, 1)
            tt(be["pick1"][:, :], be["hot1"][:, :], bank(3, NB * NE, TOK), ALU.mult).then_inc(s.r_pick, 1)
            dve.wait_ge(s.r_pick, 1)
            then(reduce(tb["pos"][:, :], by_token("pick1"), ALU.add))
            then(nc.vector.tensor_scalar(tb["kept"][:, :], tb["pos"][:, :], float(CAP), None, ALU.is_lt))
            then(tt(tb["raw"][:, :], tb["base"][:, :], tb["pos"][:, :], ALU.add))
            then(tt(tb["rel"][:, :], tb["raw"][:, :], const("spare_row", TOK), ALU.subtract))
            then(tt(tb["relk"][:, :], tb["rel"][:, :], tb["kept"][:, :], ALU.mult))
            tt(slots1[:, 0:NB], tb["relk"][:, :], const("spare_row", TOK), ALU.add).then_inc(s.r_slots_ready, 1)
            nc.vector.scalar_tensor_tensor(slots1[:, NB:], tb["pos"][:, :], float(CAP - 1), tb["base"][:, :],
                                           ALU.min, ALU.add).then_inc(s.r_slots_ready, 1)
            then(tt(tb["w"][:, :], tb["top1"][:, :], tb["kept"][:, :], ALU.mult))

            def next_rows1(e):
                after(dve, s.xe_transposed, e.n + 1)
                after(dve, s.up1_done, FC1 * e.n)
                nc.vector.tensor_copy(xeT, bank(5, KC * CAP)).then_inc(s.xeT_ready, 1)

            def down1(e):
                after(dve, s.down1_done, e.n + 1)
                for g in range(KC):
                    nc.vector.tensor_scalar(yT[:, g * CAP:(g + 1) * CAP], bank(3 + g, CAP), b2[:, ds(e.n * KC + g, 1)], None,
                                            ALU.add).then_inc(s.yT_ready, 1)

            dve.wait_ge(s.small_in, 16 * 4)
            next_rows1(beat(0, 0))
            with dve.Fori(0, NE - 1, 1) as j:
                e, nxt = Beat(j, 0, 0), Beat(j + 1, 0, 0)
                next_rows1(nxt)
                down1(e)
            down1(beat(0, NE - 1))
            for n in range(NB):
                b = beat(0, n)
                after(dve, (s.z_even, s.z_odd)[b.half], 16 * (b.pair + 1))
                nc.vector.scalar_tensor_tensor(row(x_sb, n), z_sb[b.half], tb["w"][:, n:n + 1], row(x_sb, n),
                                               ALU.mult, ALU.add).then_inc(s.out_ready, 1)

        @block.tensor
        def _(pe):
            mm, tr = nc.tensor.matmul, nc.tensor.transpose
            after(pe, s.consts_in, 16)

            def weight(n, k):
                return proj_w[:, (n * KC + k) * C:(n * KC + k + 1) * C]

            def keys(half, k, c):
                return split(ctxT[half], KC)[:, k, c * KR:(c + 1) * KR]

            def transpose_rows(bank_no, src, rows=TOK):
                for g in range(KC):
                    last = tr(bank(bank_no, rows, at=g * rows), src[:, g * P:(g + 1) * P], ident[0:rows, 0:rows])
                return last

            pe.wait_ge(s.zero_pad, 5)

            def beat_a(a, b, c):
                if a:
                    after(pe, s.xn_ready, a.n + 1)
                    after(pe, s.nrmT_ready, a.n - 1)
                    transpose_rows(4, xn).then_inc(s.xn_transposed, 1)
                    after(pe, ctx_half(a), 16 * (a.pair + 1))
                    after(pe, s.attn_w_in, 48)
                    after(pe, s.kq_biased, a.n)
                    for c3 in range(KCH):
                        for k in range(KC):
                            mm(bank(0, C, KR, at=c3 * C), keys(a.half, k, c3), weight(1, k), start=k == 0, stop=k == KC - 1)
                    after(pe, s.xnT_ready, a.n + 1)
                    for k in range(KC):
                        last = mm(bank(0, C, KR, at=KCH * C), xnT[:, k * KR:(k + 1) * KR], weight(0, k), start=k == 0, stop=k == KC - 1)
                    last.then_inc(s.kq_done, 1)
                if c:
                    after(pe, s.o_ready, c.n + 1)
                    after(pe, s.qT_ready, c.n + 1)
                    transpose_rows(5, o_sb).then_inc(s.o_transposed, 1)
                if a:
                    after(pe, s.v_copied, a.n)
                    for c3 in range(KCH):
                        for k in range(KC):
                            last = mm(bank(2, C, KR, at=c3 * C), keys(a.half, k, c3), weight(2, k), start=k == 0, stop=k == KC - 1)
                        if c3 == 0 and c:
                            project(c)
                    last.then_inc(s.v_done, 1)
                elif c:
                    project(c)
                if b:
                    after(pe, s.vr_ready, b.n + 1)
                    after(pe, s.x1_ready, b.n)
                    for g in range(KC):
                        for c3 in range(KCH):
                            rows = KR if c3 < KCH - 1 else KLAST
                            last = mm(bank(6, KV, at=g * KV), kqe[0:rows, c3 * C + g * P:c3 * C + (g + 1) * P],
                                      vr[0:rows, (c3 * KC + g) * KV:(c3 * KC + g + 1) * KV], start=c3 == 0, stop=c3 == KCH - 1)
                    last.then_inc(s.kv_done, 1)
                    after(pe, s.q_ready, b.n + 1)
                    after(pe, s.oT_ready, b.n)
                    transpose_rows(5, q_sb).then_inc(s.q_transposed, 1)
                    after(pe, s.kvm_ready, b.n + 1)
                    after(pe, s.qT_ready, b.n + 1)
                    after(pe, s.attn_scaled, KC * b.n)
                    for g in range(KC):
                        last = mm(bank(7, KV, TOK, at=g * KV), qT[:, g * TOK:(g + 1) * TOK], kvm[:, g * KV:(g + 1) * KV], start=True, stop=True)
                    last.then_inc(s.attn_done, 1)
                if c:
                    after(pe, s.nrm_ready, c.n + 1)
                    after(pe, s.xnT_ready, min(c.n + 3, NB) if isinstance(c.n, int) else c.n + 3)
                    after(pe, s.nrmT_ready, c.n + 1)
                    transpose_rows(4, nrm).then_inc(s.nrm_transposed, 1)

            def project(c):
                after(pe, s.oT_ready, c.n + 1)
                after(pe, s.kvm_ready, c.n + 1)
                for k in range(KC):
                    last = mm(bank(6, C, TOK), oT[:, k * TOK:(k + 1) * TOK], weight(3, k), start=k == 0, stop=k == KC - 1)
                last.then_inc(s.proj_done, 1)

            beat_a(beat(0, 0), None, None)
            beat_a(beat(0, 1), beat(0, 0), None)
            with pe.Fori(0, NB // 2 - 1, 1) as j:
                for k in range(2):
                    beat_a(beat(j, k + 2), beat(j, k + 1), beat(j, k))
            beat_a(None, beat(0, NB - 1), beat(0, NB - 2))
            beat_a(None, None, beat(0, NB - 1))

            def route(which, logitsT_done, logitsT_copied, logits_done):
                for h in range(2):
                    for k in range(KC):
                        last = mm(bank(h, HT, NE), routers[:, (which * KC + k) * NE:(which * KC + k + 1) * NE],
                                  rowsT[:, k * NT + h * HT:k * NT + (h + 1) * HT], start=k == 0, stop=k == KC - 1)
                    last.then_inc(logitsT_done, 1)
                after(pe, logitsT_copied, 2)
                for n in range(NB):
                    last = tr(bank(2, NE, TOK, at=n * NE), logitsT[:, n * TOK:(n + 1) * TOK], ident[0:NE, 0:NE])
                last.then_inc(logits_done, 1)

            def ranks(done):
                for n in range(NB):
                    mm(bank(3, (NB - n) * NE, at=(n + 1) * NE), const("ones", TOK),
                       hots[:, n * NE:(n + 1) * NE].unsqueeze(1).to_broadcast([TOK, NB - n, NE]),
                       start=n == 0, stop=False, skip_group_check=True)
                last = mm(bank(3, (NB + 1) * NE), const("earlier", TOK), hots[:, :], start=False, stop=True, skip_group_check=True)
                last.then_inc(done, 1)

            after(pe, s.nrmT_ready, NB + 1)
            after(pe, s.small_in, 16 * 4)
            route(0, s.logitsT_done, s.logitsT_copied, s.logits_done)

            def shared_up(h):
                for g in range(KC):
                    for part in range(2):
                        o = bank(4 * h + 2 * g + part, HT)
                        for k in range(KC):
                            at = k * 2 * FFS + part * FFS + g * P
                            last = mm(o, shared_w[:, at:at + P], rowsT[:, k * NT + h * HT:k * NT + (h + 1) * HT], start=k == 0, stop=k == KC - 1)
                    last.then_inc(s.sh_up_done, 1)

            shared_up(SHARED_ORDER[0])
            after(pe, s.both_hot, 1)
            ranks(s.rank_done)
            after(pe, s.rank_copied, 1)
            shared_up(SHARED_ORDER[1])
            for n in range(NB):
                after(pe, s.sh_hid, 2 * KC)
                after(pe, s.x1s_ready, n - 3)
                for k in range(KC):
                    last = mm(bank(n % 4, C, TOK), sh_hT[:, k * NT + n * TOK:k * NT + (n + 1) * TOK],
                              shared_w[:, KC * 2 * FFS + k * C:KC * 2 * FFS + (k + 1) * C], start=k == 0, stop=k == KC - 1)
                last.then_inc(s.sh_down_done, 1)

            def rows_in(i):
                after(pe, (s.xg_even, s.xg_odd)[i.half], 16 * (i.pair + 1))
                after(pe, s.xgT_ready, i.n)
                transpose_rows(6, xg[i.half], P).then_inc(s.xg_transposed, 1)

            def gate_up(i):
                off = pe.value_load(tile_off[0:1, ds(i.n, 1)], min_val=0, max_val=(NE - 1) * EW)
                after(pe, s.xgT_ready, i.n + 1)
                for j3 in range(3):
                    after(pe, s.h_ready, 3 * i.n + j3 - 2)
                    for k in range(KC):
                        last = mm(bank(j3), xgT[:, k * P:(k + 1) * P], wres[:, ds(off + (k * GU + j3 * BANK), BANK)], start=k == 0, stop=k == KC - 1)
                    last.then_inc(s.gu_done, 1)
                return off

            def down(i):
                off = pe.value_load(tile_off[0:1, ds(i.n, 1)], min_val=0, max_val=(NE - 1) * EW)
                after(pe, s.hT_lo, i.n + 1)
                after(pe, s.hT_hi, i.n + 1)
                for k in range(FC0):
                    last = mm(bank(5, C), hT[:, k * P:(k + 1) * P], wres[:, ds(off + (KC * GU + k * C), C)], start=k == 0, stop=k == FC0 - 1)
                last.then_inc(s.down_done, 1)

            def transpose_hidden(i):
                for half in range(2):
                    after(pe, (s.hT_lo, s.hT_hi)[half], i.n)
                    for m in range(FC0 // 2):
                        k = half * (FC0 // 2) + m
                        after(pe, s.h_ready, 3 * i.n + k // 2 + 1)
                        last = tr(bank(3 + half, P, at=m * P), h_sb[:, k * P:(k + 1) * P], ident)
                    last.then_inc(s.h_transposed, 1)

            after(pe, s.tile_off, 1)
            after(pe, s.experts_in, 16 * NE)
            after(pe, s.x1s_ready, NB)
            rows_in(beat(0, 0))
            gate_up(beat(0, 0))
            transpose_hidden(beat(0, 0))
            rows_in(beat(0, 1))
            with pe.Fori(0, TILES // 2 - 1, 1) as j:
                for k in range(1, 3):
                    gate_up(beat(j, k))
                    down(beat(j, k - 1))
                    transpose_hidden(beat(j, k))
                    rows_in(beat(j, k + 1))
            gate_up(beat(0, TILES - 1))
            down(beat(0, TILES - 2))
            transpose_hidden(beat(0, TILES - 1))
            down(beat(0, TILES - 1))

            after(pe, s.wx_in, 32)

            def beat_c(a, b, c):
                if b:
                    after(pe, s.xn3_ready, b.n + 1)
                    after(pe, s.xn4T_ready, b.n)
                    transpose_rows(4, xn3).then_inc(s.xn3_transposed, 1)
                if a:
                    after(pe, (s.ctx2_even, s.ctx2_odd)[a.half], 16 * (a.pair + 1))
                    after(pe, s.kT_ready, KC * a.n)
                    for g in range(KC):
                        for k in range(KC):
                            last = mm(bank(g, KEYS), wx[:, k * C + g * P:k * C + (g + 1) * P], ctxT2[a.half][:, k * KEYS:(k + 1) * KEYS],
                                      start=k == 0, stop=k == KC - 1)
                    last.then_inc(s.kT_done, 1)
                if b:
                    after(pe, s.xn3T_ready, b.n + 1)
                    after(pe, s.pT_ready, b.n)
                    for g in range(KC):
                        for k in range(KC):
                            last = mm(bank(5, TOK, at=g * TOK), wx[:, k * C + g * P:k * C + (g + 1) * P], xn3T[:, k * TOK:(k + 1) * TOK],
                                      start=k == 0, stop=k == KC - 1)
                    last.then_inc(s.q1_done, 1)
                if c:
                    after(pe, s.xn4_made, c.n + 1)
                    after(pe, s.xn3T_ready, min(c.n + 2, NB) if isinstance(c.n, int) else c.n + 2)
                    after(pe, s.xn4T_ready, c.n + 1)
                    transpose_rows(4, xn4).then_inc(s.xn4_transposed, 1)
                if b:
                    after(pe, s.q1T_ready, KC * (b.n + 1))
                    after(pe, s.p_ready, b.n)
                    for k in range(KC):
                        last = mm(bank(6, KEYS, TOK), q1T[:, k * TOK:(k + 1) * TOK], kT[b.half][:, k * KEYS:(k + 1) * KEYS],
                                  start=k == 0, stop=k == KC - 1)
                    last.then_inc(s.score_done, 1)
                if a:
                    after(pe, s.kT_ready, KC * (a.n + 1))
                    after(pe, s.vn_ready, a.n)
                    for c3 in range(KCH):
                        rows = KR if c3 < KCH - 1 else KLAST
                        for g in range(KC):
                            last = tr(bank(2, P, rows, at=c3 * C + g * P), kT[a.half][:, g * KEYS + c3 * KR:g * KEYS + c3 * KR + rows], ident)
                    last.then_inc(s.vT_done, 1)
                if b:
                    after(pe, s.p_ready, b.n + 1)
                    for c3 in range(KCH):
                        rows = KR if c3 < KCH - 1 else KLAST
                        last = tr(bank(5, TOK, rows, at=c3 * TOK), p_sb[:, c3 * KR:c3 * KR + rows], ident[0:TOK, 0:TOK])
                    last.then_inc(s.p_transposed, 1)
                    after(pe, s.pT_ready, b.n + 1)
                    after(pe, s.x3_ready, b.n)
                    for c3 in range(KCH):
                        rows = KR if c3 < KCH - 1 else KLAST
                        last = mm(bank(7, C, TOK), pT[0:rows, c3 * TOK:(c3 + 1) * TOK], v_nat[0:rows, c3 * C:(c3 + 1) * C],
                                  start=c3 == 0, stop=c3 == KCH - 1)
                    last.then_inc(s.av_done, 1)

            beat_c(beat(0, 0), None, None)
            beat_c(beat(0, 1), beat(0, 0), None)
            with pe.Fori(0, NB // 2 - 1, 1) as j:
                for k in range(2):
                    beat_c(beat(j, k + 2), beat(j, k + 1), beat(j, k))
            beat_c(None, beat(0, NB - 1), beat(0, NB - 2))
            beat_c(None, None, beat(0, NB - 1))

            after(pe, s.xn4T_ready, NB + 1)
            route(1, s.r_logitsT_done, s.r_logitsT_copied, s.r_logits_done)
            after(pe, s.r_hots, 1)
            ranks(s.r_rank_done)
            after(pe, s.r_pick, 1)

            def rows_in1(e):
                after(pe, (s.xe_even, s.xe_odd)[e.half], 16 * (e.pair + 1))
                after(pe, s.xeT_ready, e.n)
                for k in range(KC):
                    for m in range(2):
                        last = tr(bank(5, HALF, at=k * CAP + m * HALF), xe[e.half][:, m * C + k * P:m * C + (k + 1) * P], ident[0:HALF, 0:HALF])
                last.then_inc(s.xe_transposed, 1)

            def rows_out1(e):
                after(pe, s.yT_ready, KC * (e.n + 1))
                for m in range(2):
                    for g in range(KC):
                        last = tr(bank(6, P, HALF, at=m * C + g * P), yT[:, g * CAP + m * HALF:g * CAP + (m + 1) * HALF], ident)
                last.then_inc(s.yT_transposed, 1)

            def expert(e, last_e, nxt):
                after(pe, (s.w1_even, s.w1_odd)[e.half], 16 * (e.pair + 1))
                after(pe, s.xeT_ready, e.n + 1)
                for j8 in range(FC1):
                    after(pe, s.gelu_done, FC1 * e.n + j8 - 2)
                    for k in range(KC):
                        last = mm(bank(j8 % 3, CAP), w1[e.half][:, k * FF1 + j8 * P:k * FF1 + (j8 + 1) * P], xeT[:, k * CAP:(k + 1) * CAP],
                                  start=k == 0, stop=k == KC - 1)
                    last.then_inc(s.up1_done, 1)
                if last_e:
                    rows_out1(last_e)
                if nxt:
                    rows_in1(nxt)
                after(pe, (s.w2_even, s.w2_odd)[e.half], 16 * (e.pair + 1))
                after(pe, s.yT_ready, KC * e.n)
                for j8 in range(FC1):
                    after(pe, s.gelu_done, FC1 * e.n + j8 + 1)
                    for g in range(KC):
                        last = mm(bank(3 + g, CAP), w2[e.half][:, j8 * C + g * P:j8 * C + (g + 1) * P], hidT[:, j8 * CAP:(j8 + 1) * CAP],
                                  start=j8 == 0, stop=j8 == FC1 - 1)
                last.then_inc(s.down1_done, 1)

            rows_in1(beat(0, 0))
            expert(beat(0, 0), None, beat(0, 1))
            with pe.Fori(0, NE // 2 - 1, 1) as j:
                for k in range(1, 3):
                    expert(beat(j, k), beat(j, k - 1), beat(j, k + 1))
            expert(beat(0, NE - 1), beat(0, NE - 2), None)
            after(pe, s.y1_copied, NE - 1)
            rows_out1(beat(0, NE - 1))


def _chunks(w):
    k, n = w.shape
    return w.reshape(k // P, P, n).transpose(1, 0, 2).reshape(P, -1)


def kernel(**inputs):
    import numpy as _np
    import concourse.bacc as _bacc
    from concourse import mybir as _mybir
    from concourse.bass_utils import run_bass_kernel_spmd as _run

    a = {k: _np.asarray(v) for k, v in inputs.items()}
    gu = a["L0_ffn_gate_up_w"].transpose(0, 2, 1).reshape(NE, KC, P, 2, 3, C).transpose(0, 2, 1, 4, 3, 5).reshape(NE, P, KC * GU)
    dn = a["L0_ffn_down_w"].transpose(0, 2, 1).reshape(NE, FC0, P, C).transpose(0, 2, 1, 3).reshape(NE, P, FC0 * C)
    wide = lambda rows: _np.tile(_np.concatenate([a[n] for n in rows])[None, :], (P, 1))
    arrays = {
        "x": a["x"].transpose(1, 0, 2).reshape(TOK, NB * C),
        "ctx": a["ctx_1024"].transpose(0, 2, 1).reshape(NB, KC, P, KEYS).transpose(0, 2, 1, 3).reshape(NB, P, KC * KEYS),
        "proj_w": _np.concatenate([_chunks(a[n].T) for n in ("L0_xattn_Wq", "L0_xattn_Wk", "L0_xattn_Wv", "L0_xattn_Wp")], axis=1),
        "bias": wide(["L0_xattn_bk"] * KCH + ["L0_xattn_bq"]),
        "rows": wide(["L0_xattn_bv", "L0_xattn_bp", "L0_ffn_ln_gamma", "L0_ffn_ln_beta"]),
        "routers": _np.concatenate([_chunks(a["L0_ffn_router_w"].T), _chunks(a["L1_ffn_router_w"].T)], axis=1),
        "shared_w": _np.concatenate([_chunks(a["L0_ffn_shared_gate_up_w"].T), _chunks(a["L0_ffn_shared_down_w"].T)], axis=1),
        "experts": _np.concatenate([gu, dn], axis=2),
        "wx": _chunks(a["L1_xattn_W"].T),
        "bx": a["L1_xattn_b"].reshape(KC, P).T,
        "w1": a["L1_ffn_w1"].reshape(NE, KC, P, FF1).transpose(0, 2, 1, 3).reshape(NE, P, KC * FF1),
        "b1": a["L1_ffn_b1"].reshape(NE * FC1, P).T,
        "w2": a["L1_ffn_w2"].reshape(NE, FC1, P, C).transpose(0, 2, 1, 3).reshape(NE, P, FC1 * C),
        "b2": a["L1_ffn_b2"].reshape(NE * KC, P).T,
        "consts": constants(),
    }
    arrays = {k: _np.ascontiguousarray(v) for k, v in arrays.items()}
    nc = _bacc.Bacc("TRN2", target_bir_lowering=False, num_devices=1)
    args = [nc.dram_tensor("in_" + k, v.shape, _mybir.dt.from_np(v.dtype), kind="ExternalInput").ap() for k, v in arrays.items()]
    out = nc.dram_tensor("out_0", (NB, TOK, C), _mybir.dt.float32, kind="ExternalOutput").ap()
    two_layers(nc, *args, out)
    r = _run(nc, [{"in_" + k: v for k, v in arrays.items()}], core_ids=[0])
    return r.results[0]["out_0"]
```

```python
import math
from collections import namedtuple
from contextlib import ExitStack

import numpy as np

import concourse.bass as bass
from concourse import mybir

NB, TOK, C = 8, 100, 256
KEYS = 361
HEADS = 16
HD = C // HEADS
KC = 2
P = 128
NE = 8
KCH = 3
KR = -(-KEYS // KCH)
KLAST = KEYS - (KCH - 1) * KR
FF0 = 768
FFS = 256
GU = 2 * FF0
FC0 = FF0 // P
EW = KC * GU + FC0 * C
TOPK = 2
TILES = (TOPK * NB * TOK + NE * (P - 1)) // P
SLOTS = TILES * P
FF1 = 1024
FC1 = FF1 // P
CAP = math.ceil(1.5 * NB * TOK / NE)
HALF = CAP // 2
ROWS1 = NE * CAP + NB * TOK
HG = HEADS // KC
KV = P + HG
NT = NB * TOK
HT = NT // 2
LOGIT_PARTS = ((0, NB // 2), (NB // 2, NB - 1), (NB - 1, NB))
SHARED_ORDER = (1, 0)
EPS = 1e-5
MOMENTS = 3
BANK = 512

CONST = [("ident", P), ("headmask", KC * KV), ("earlier", P), ("ones", P), ("expert_m", NB * NE),
         ("tile_edge", NE * (TILES // 2)), ("tile_no", TILES), ("cap_base", NB * NE), ("spare_row", NB), ("minus_half", 1),
         ("zero", C)]
CONST_AT = {}
_at = 0
for _n, _w in CONST:
    CONST_AT[_n] = (_at, _w)
    _at += _w
CONST_W = _at


def constants():
    c = {n: np.zeros((P, w), np.float32) for n, w in CONST}
    c["ident"][:] = np.eye(P)
    part_head = np.arange(P) // HD
    for g in range(KC):
        c["headmask"][:, g * KV:g * KV + P] = part_head[:, None] == part_head[None, :]
        c["headmask"][:, g * KV + P:(g + 1) * KV] = part_head[:, None] == np.arange(HG)[None, :]
    t = np.arange(P)
    c["earlier"][:] = (t[:, None] < t[None, :]) & (t[None, :] < TOK) & (t[:, None] < TOK)
    c["ones"][:] = 1.0
    c["expert_m"][:] = np.tile(np.arange(NE) - NE, NB)
    c["tile_edge"][:] = np.tile(P * np.arange(TILES // 2), NE)
    c["tile_no"][:] = np.arange(TILES)
    c["cap_base"][:] = np.tile(CAP * np.arange(NE), NB)
    c["spare_row"][:] = NE * CAP + TOK * np.arange(NB)[None, :] + t[:, None]
    c["minus_half"][:] = -0.5
    return np.concatenate([c[n] for n, _ in CONST], axis=1)


def after(eng, sem, n):
    if isinstance(n, int) and n <= 0:
        return
    eng.wait_ge(sem, n)


def after_alone(eng, sem, n):
    after(eng, sem, n)
    if not isinstance(n, int):
        eng.nop(nofuse=True)


Beat = namedtuple("Beat", "n half pair")


def is_last(b):
    return isinstance(b.n, int) and b.n == NB - 1


def beat(j, k):
    return Beat(2 * j + k, k % 2, j + k // 2)


SEMS = """
x0_in x_in consts_in wk_in attn_w_in bias_in ctx_even ctx_odd small_in experts_in zeroed
moments0 rstd0 xn_ready xn_transposed xnT_ready
kq_done kq_biased kq_max kq_centered kq_exp v_done v_copied kq_sum kq_recip q_ready vr_ready
kv_done kvm_ready q_transposed qT_ready attn_done den_recip attn_scaled q_plus_bv o_ready o_transposed oT_ready
proj_done x_plus_bp x1_ready
moments1 rstd1 n1_ready moments2 rstd2 n2_ready scaled_by_gamma nrm_ready nrm_kept nrm_transposed nrmT_ready
zero_pad
logitsT_done logitsT_copied logits_done centred exponentials routing_step gap gap_exp both_hot rank_done rank_copied
tile_off slots_ready scattered
sh_up_done sh_silu sh_hid sh_down_done x1s_ready
xg_even xg_odd xg_transposed xgT_ready gu_done silu_done h_ready h_transposed hT_lo hT_hi down_done y_copied y_even y_odd
yg_0 yg_1 yg_2 yg_3 wx_in keys2_done keys2_copied keys2_stored wx_back kT_even kT_odd
comb1 x2_ready moments3 rstd3 xn3_ready xn3_transposed xn3T_ready
vT_done vn_ready q1_done q1T_ready score_done score_max neg_max p_ready p_recip p_transposed pT_ready
av_done x3_ready moments4 rstd4 xn4_made xn4_ready xn4_transposed xn4T_ready
r_logitsT_done r_logitsT_copied r_logits_done r_centred r_exponentials r_hots r_rank_done
r_pick r_slots_ready r_scattered
w1_even w1_odd w2_even w2_odd xe_even xe_odd xe_transposed xeT_ready up1_done gelu_done down1_done yT_ready yT_transposed
y1_copied y1_even y1_odd z_first z_second out_ready out_stored
""".split()
Sems = namedtuple("Sems", SEMS)


def two_layers(nc, x_d, ctx_d, proj_w_d, bias_d, rows_d, routers_d, shared_w_d, experts_d, wx_d, bx_d,
               w1_d, b1_d, w2_d, b2_d, consts_d, out_d):
    f32, u32, i32 = mybir.dt.float32, mybir.dt.uint32, mybir.dt.int32
    ACT, ALU, AX = mybir.ActivationFunctionType, mybir.AluOpType, mybir.AxisListType
    ds = bass.ds
    ctx = ExitStack()
    with ctx:
        def sb(name, cols, dt=f32, rows=P):
            return ctx.enter_context(nc.sbuf_tensor(name, [rows, cols], dt))

        s = Sems(*[ctx.enter_context(nc.semaphore(n)) for n in SEMS])

        xg_dram = nc.dram_tensor("rows_by_slot0", (SLOTS, C), f32, kind="Internal").ap()
        yg_dram = nc.dram_tensor("results_by_slot0", (SLOTS, C), f32, kind="Internal").ap()
        xe_dram = nc.dram_tensor("rows_by_slot1", (ROWS1, C), f32, kind="Internal").ap()
        kT_dram = nc.dram_tensor("keys_of_layer1", (NB, P, KC * KEYS), f32, kind="Internal").ap()
        ye_dram = nc.dram_tensor("results_by_slot1", (NE * CAP, C), f32, kind="Internal").ap()

        wres = sb("wres", NE * EW)
        YG = 4
        LATE = 2

        class Region:
            def __init__(self, lo, hi, over=wres):
                self.at, self.hi, self.over = lo, hi, over

            def take(self, cols, rows=P):
                ap = self.over[0:rows, self.at:self.at + cols]
                self.at += cols
                assert self.at <= self.hi
                return ap

        ra = Region((NE - LATE) * EW, NE * EW)
        proj_w = ra.take(4 * KC * C)
        bias4 = ra.take(4 * C)
        rows4 = ra.take(4 * C)
        ctxT = [ra.take(KC * KCH * KR) for _ in range(2)]
        kq = ra.take(4 * C, KR)
        kqe = ra.take(4 * C, KR)
        v_sb = ra.take(KCH * C, KR)
        vr = ra.take(KCH * KC * KV, KR)

        rc = Region(0, NE * EW)
        v_nat = [rc.take(KCH * C, KR) for _ in range(2)]
        q1T = rc.take(KC * TOK)
        xn3 = rc.take(C, TOK)
        xn3T = rc.take(KC * TOK)
        p_sb = rc.take(KCH * KR, TOK)
        pT = rc.take(KCH * TOK, KR)
        yg = [rc.take(TOPK * C, TOK) for _ in range(YG)]
        xn4 = rc.take(C, TOK)
        w1 = [rc.take(KC * FF1) for _ in range(2)]
        w2 = [rc.take(FC1 * C) for _ in range(2)]
        xe = [rc.take(2 * C, HALF) for _ in range(2)]
        xeT = rc.take(KC * CAP)
        hidT = rc.take(FC1 * CAP)
        yT = rc.take(KC * CAP)
        y1 = [rc.take(2 * C, HALF) for _ in range(2)]
        z_sb = rc.take(NB * C, TOK)

        consts = sb("consts", CONST_W)

        def const(name, rows=P):
            at, w = CONST_AT[name]
            return consts[0:rows, at:at + w]

        x_sb = sb("x_sb", NB * C, rows=TOK)
        rows_sb = sb("rows_sb", NB * C, rows=TOK)
        rowsT = sb("rowsT", KC * NT)
        routers = sb("routers", 2 * KC * NE)
        b1 = sb("b1", NE * FC1)
        b2 = sb("b2", NE * KC)
        shared_w = sb("shared_w", KC * 2 * FFS + KC * C)
        sh_hT = sb("sh_hT", KC * NT)
        wx_a = sh_hT[:, 0:KC * C]
        keys2 = sh_hT[:, KC * C:KC * (C + KEYS)]
        bx = sb("bx", KC)
        wx = shared_w[:, 0:KC * C]
        kT = [shared_w[:, KC * C:KC * (C + KEYS)], sh_hT[:, 0:KC * KEYS]]
        work = sb("work", 2 * C + KC * P + 3 * FF0 + 2 * C)
        rt = Region(0, work.shape[1], work)
        xg = [rt.take(C) for _ in range(2)]
        xgT = rt.take(KC * P)
        sg = rt.take(FF0)
        h_sb = rt.take(FF0)
        hT = rt.take(FF0)
        y_sb = [rt.take(C) for _ in range(2)]
        logitsT = work[0:NE, 0:NT]
        sh_sg = work[:, NT:NT + KC * HT]
        rs = Region(0, work.shape[1], work)
        xn = rs.take(C, TOK)
        xnT = rs.take(KC * KR)
        q_sb = rs.take(C, TOK)
        q_bv = rs.take(C, TOK)
        qT = rs.take(KC * TOK)
        kvm = rs.take(KC * KV)
        o1 = rs.take(C, TOK)
        o_sb = rs.take(C, TOK)
        oT = rs.take(KC * TOK)
        xbp = rs.take(C, TOK)
        n1 = rs.take(C, TOK)
        n2 = rs.take(C, TOK)
        nrm = rs.take(C, TOK)
        kq_m = sb("kq_m", 4 * HEADS, rows=KR)
        kq_s = sb("kq_s", 4 * HEADS, rows=KR)
        kq_r = sb("kq_r", 4 * HEADS, rows=KR)
        den = sb("den", KC * HG, rows=TOK)
        bn = [sb(f"bn{i}", 6, rows=TOK) for i in range(5)]
        mv = [sb(f"mv{i}", 2, rows=TOK) for i in range(5)]
        ve = [sb(f"ve{i}", 1, rows=TOK) for i in range(5)]
        rstd = [sb(f"rstd{i}", 1, rows=TOK) for i in range(5)]
        p_max = sb("p_max", 1, rows=TOK)
        p_neg = sb("p_neg", 1, rows=TOK)
        p_sum = sb("p_sum", 1, rows=TOK)
        p_rec = sb("p_rec", 1, rows=TOK)
        be = {n: sb("rt_" + n, NB * NE, rows=TOK) for n in "cent exp probs eq eqm hot1 masked hot2 rows pick1 pick2".split()}
        tb = {n: sb("rt_" + n, NB, rows=TOK) for n in "max sum rec idx top1 top2 gap egap gden g1 g2 slot1 slot2 pos base kept raw rel relk w".split()}
        PAD = NB // 2
        sums = [sb(f"choices{w}", (PAD + NB + 2) * NE, rows=TOK) for w in (1, 2, 4, 8)]

        def blocks(w, first, n):
            return sums[w][:, first * NE:(first + n) * NE]

        hots = blocks(0, PAD + 1, NB + 1)
        rank = sb("rank", (NB + 1) * NE)
        over_edge = sb("over_edge", NE * (TILES // 2))
        tiles_n = sb("tiles_n", NE)
        tiles_scan = sb("tiles_scan", NE)
        first_tile = sb("first_tile", NE)
        base_row = sb("base_row", NE)
        zero8 = sb("zero8", NE)
        tile_cmp = sb("tile_cmp", TILES * NE, rows=1)
        tile_expert = sb("tile_expert", TILES, rows=1)
        tile_off = sb("tile_off", TILES, i32, rows=1)
        slots0 = sb("slots0", TOPK * NB, u32, rows=TOK)
        slots1 = sb("slots1", 2 * NB, u32, rows=TOK)

        psum = ctx.enter_context(nc.psum_tensor("psum", [P, 8 * BANK], f32))

        def bank(n, cols=BANK, rows=P, at=0):
            return psum[0:rows, n * BANK + at:n * BANK + at + cols]

        ident = const("ident")

        def split(ap, n):
            return ap.rearrange("p (n m) -> p n m", n=n)

        def each(ap, m):
            return ap.unsqueeze(2).to_broadcast([ap.shape[0], ap.shape[1], m])

        def row(t, n, w=C):
            return t[:, ds(n * w, w)]

        def ctx_half(b):
            return (s.ctx_even, s.ctx_odd)[b.half]

        def run_beats(eng, step):
            def peeled(t):
                step(*[beat(0, t - back) if 0 <= t - back < NB else None for back in range(4)])

            for t in range(3):
                peeled(t)
            with eng.Fori(0, (NB - 3) // 2, 1) as j:
                for k in range(3, 5):
                    step(*[beat(j, k - back) for back in range(4)])
            for t in range(NB - 1, NB + 3):
                peeled(t)

        def run_beats_c(eng, step):
            def peeled(t):
                step(*[beat(0, t - back) if 0 <= t - back < NB else None for back in range(3)])

            peeled(0)
            peeled(1)
            with eng.Fori(0, (NB - 2) // 2, 1) as j:
                for k in range(2, 4):
                    step(*[beat(j, k - back) for back in range(3)])
            peeled(NB)
            peeled(NB + 1)

        block = ctx.enter_context(nc.Block())

        @block.sync
        def _(sp):
            def load_ctx(b):
                sp.dma_start(split(ctxT[b.half], KC)[:, :, 0:KEYS],
                             ctx_d[ds(b.n, 1)].rearrange("b p (k n) -> (b p) k n", k=KC)).then_inc(ctx_half(b), 16)

            def load_weights(lo, hi, sem):
                at = slice(lo * KC * C, hi * KC * C)
                sp.dma_start(proj_w[:, at], proj_w_d[:, at]).then_inc(sem, 16)

            load_ctx(beat(0, 0))
            load_weights(1, 2, s.wk_in)
            load_weights(2, 4, s.attn_w_in)
            load_weights(0, 1, s.attn_w_in)
            sp.dma_start(bias4, bias_d).then_inc(s.bias_in, 16)
            sp.dma_start(x_sb[:, C:], x_d[:, C:]).then_inc(s.x_in, 16)
            sp.dma_start(bx[:, :], bx_d).then_inc(s.wx_in, 16)
            sp.dma_start(wx_a, wx_d).then_inc(s.wx_in, 16)
            sp.dma_start(rows4, rows_d).then_inc(s.bias_in, 16)
            load_ctx(beat(0, 1))

            def load_expert(n):
                sp.dma_start(wres[:, ds(n * EW, EW)], experts_d[ds(n, 1)].rearrange("e p n -> (e p) n")).then_inc(s.experts_in, 16)

            def store_keys(b):
                after(sp, s.keys2_copied, KC * (b.n + 1))
                sp.dma_start(kT_dram[ds(b.n, 1)].rearrange("b p n -> (b p) n"), keys2).then_inc(s.keys2_stored, 16)

            with sp.Fori(0, NB // 2 - 1, 1) as j:
                for k in range(2):
                    b = beat(j, k)
                    load_expert(b.n)
                    after(sp, s.keys2_done, KC * (b.n + 1))
                    after(sp, s.v_done, b.n + 1)
                    load_ctx(beat(j, k + 2))
                    store_keys(b)
            for n in range(NB - 2, NB):
                store_keys(beat(0, n))
            sp.dma_start(shared_w[:, :], shared_w_d).then_inc(s.small_in, 16)
            sp.dma_start(routers[:, :], routers_d).then_inc(s.small_in, 16)
            sp.dma_start(b1[:, :], b1_d).then_inc(s.small_in, 16)
            sp.dma_start(b2[:, :], b2_d).then_inc(s.small_in, 16)
            after(sp, s.proj_done, NB)
            after(sp, s.nrm_ready, NB)
            for n in range(NE - LATE, NE):
                load_expert(n)

            def load_rows0(i):
                half = (s.xg_even, s.xg_odd)[i.half]
                sp.dma_start(xg[i.half], xg_dram[ds(i.n * P, P), :]).then_inc(half, 16)

            after(sp, s.scattered, 16 * TOPK * NB)
            load_rows0(beat(0, 0))
            load_rows0(beat(0, 1))

            def load_kT(b):
                sp.dma_start(kT[b.half], kT_dram[ds(b.n, 1)].rearrange("b p n -> (b p) n")).then_inc((s.kT_even, s.kT_odd)[b.half], 16)

            after(sp, s.sh_down_done, NB)
            after(sp, s.keys2_stored, 16 * NB)
            sp.dma_start(wx, wx_d).then_inc(s.wx_back, 16)
            load_kT(beat(0, 0))
            load_kT(beat(0, 1))
            with sp.Fori(0, TILES // 2 - 1, 1) as j:
                for k in range(2):
                    i = beat(j, k)
                    after(sp, s.xg_transposed, i.n + 1)
                    load_rows0(beat(j, k + 2))

            def load_w1(e):
                sp.dma_start(w1[e.half], w1_d[ds(e.n, 1)].rearrange("e p n -> (e p) n")).then_inc((s.w1_even, s.w1_odd)[e.half], 16)

            def load_w2(e):
                sp.dma_start(w2[e.half], w2_d[ds(e.n, 1)].rearrange("e p n -> (e p) n")).then_inc((s.w2_even, s.w2_odd)[e.half], 16)

            with sp.Fori(0, NB // 2 - 1, 1) as j:
                for k in range(2):
                    after(sp, s.score_done, beat(j, k).n + 1)
                    load_kT(beat(j, k + 2))
            after(sp, s.x2_ready, NB)
            for k in range(2):
                load_w1(beat(0, k))
                load_w2(beat(0, k))

            def load_rows1(e):
                sp.dma_start(split(xe[e.half], 2), xe_dram[ds(e.n * CAP, CAP), :].rearrange("(m p) c -> p m c", p=HALF)).then_inc((s.xe_even, s.xe_odd)[e.half], 16)

            after(sp, s.r_scattered, 16 * NB)
            load_rows1(beat(0, 0))
            load_rows1(beat(0, 1))
            with sp.Fori(0, NE // 2 - 1, 1) as j:
                for k in range(2):
                    e = beat(j, k)
                    after(sp, s.xe_transposed, e.n + 1)
                    load_rows1(beat(j, k + 2))
                    after(sp, s.up1_done, FC1 * (e.n + 1))
                    load_w1(beat(j, k + 2))
                    after(sp, s.down1_done, e.n + 1)
                    load_w2(beat(j, k + 2))
            for n in range(NB):
                after(sp, s.out_ready, n + 1)
                sp.dma_start(out_d[n, :, :], row(x_sb, n)).then_inc(s.out_stored, 16)
            sp.wait_ge(s.out_stored, 16 * NB)

        @block.gpsimd
        def _(pool):
            def tt(out, a, b, op):
                return nc.gpsimd.tensor_tensor(out, a, b, op)

            def inverse_deviation(kind, n, steps, rstd_sem):
                after(pool, steps, MOMENTS * (n + 1))
                tt(rstd[kind][:, :], ve[kind][:, :], const("minus_half", TOK), ALU.pow).then_inc(rstd_sem, 1)

            def clear_slots():
                zeros = const("zero")
                pool.dma_start(xg_dram.rearrange("(p s) c -> p s c", p=P),
                               zeros.unsqueeze(1).to_broadcast([P, SLOTS // P, C])).then_inc(s.zeroed, 16)
                pool.dma_start(xe_dram[0:NE * CAP, :].rearrange("(p s) c -> p s c", p=NE * CAP // 10),
                               zeros[0:NE * CAP // 10, :].unsqueeze(1).to_broadcast([NE * CAP // 10, 10, C])).then_inc(s.zeroed, 16)

            def beat_a(a, b, c, d):
                if c:
                    after(pool, s.x1_ready, c.n)
                    tt(xbp, row(x_sb, c.n), rows4[0:TOK, C:2 * C], ALU.add).then_inc(s.x_plus_bp, 1)
                if b:
                    after(pool, s.kq_recip, b.n + 1)
                    after(pool, s.q_transposed, b.n)
                    tt(split(q_sb, HEADS), split(kqe[0:TOK, 3 * C:4 * C], HEADS),
                       each(kq_r[0:TOK, 3 * HEADS:4 * HEADS], HD), ALU.mult).then_inc(s.q_ready, 1)
                    after(pool, s.o_ready, b.n)
                    pool.wait_ge(s.q_ready, b.n + 1)
                    tt(q_bv, q_sb, rows4[0:TOK, 0:C], ALU.add).then_inc(s.q_plus_bv, 1)
                if d:
                    inverse_deviation(2, d.n, s.moments2, s.rstd2)
                if a and not is_last(a):
                    inverse_deviation(0, a.n + 1, s.moments0, s.rstd0)
                if d:
                    after(pool, s.n2_ready, d.n + 1)
                    tt(n2, n2, rows4[0:TOK, 2 * C:3 * C], ALU.mult).then_inc(s.scaled_by_gamma, 1)
                    after(pool, s.nrmT_ready, d.n + 1)
                    pool.wait_ge(s.scaled_by_gamma, d.n + 1)
                    tt(nrm, n2, rows4[0:TOK, 3 * C:4 * C], ALU.add).then_inc(s.nrm_ready, 1)
                if a:
                    after(pool, s.kq_max, a.n + 1)
                    tt(split(kq, 4 * HEADS), split(kq, 4 * HEADS), each(kq_m[:, :], HD), ALU.subtract).then_inc(s.kq_centered, 1)
                if c:
                    inverse_deviation(1, c.n, s.moments1, s.rstd1)
                if a and is_last(a):
                    clear_slots()

            after(pool, s.consts_in, 16)
            inverse_deviation(0, 0, s.moments0, s.rstd0)

            after(pool, s.x_in, 16)
            after(pool, s.bias_in, 32)
            run_beats(pool, beat_a)

            pool.wait_ge(s.zeroed, 32)
            pool.wait_ge(s.nrm_kept, NB)
            for k in range(TOPK):
                pool.wait_ge(s.slots_ready, k + 1)
                for n in range(NB):
                    nc.gpsimd.indirect_dma_start(
                        out=xg_dram, out_offset=bass.IndirectOffsetOnAxis(ap=slots0[:, k * NB + n:k * NB + n + 1], axis=0),
                        in_=rows_sb[:, n * C:(n + 1) * C], in_offset=None).then_inc(s.scattered, 16)

            after(pool, s.y_even, 16 * (TILES // 2 + 1))
            after(pool, s.y_odd, 16 * (TILES // 2 + 1))
            after(pool, s.down_done, TILES)

            def gather(n):
                after(pool, s.x2_ready, n - YG + 1)
                for k in range(TOPK):
                    nc.gpsimd.indirect_dma_start(
                        out=yg[n % YG][:, k * C:(k + 1) * C], out_offset=None, in_=yg_dram,
                        in_offset=bass.IndirectOffsetOnAxis(ap=slots0[:, k * NB + n:k * NB + n + 1], axis=0)
                    ).then_inc((s.yg_0, s.yg_1, s.yg_2, s.yg_3)[n % YG], 16)

            for n in range(YG - 1):
                gather(n)
            for n in range(NB + 2):
                if n < NB:
                    inverse_deviation(3, n, s.moments3, s.rstd3)
                    if n + YG - 1 < NB:
                        gather(n + YG - 1)
                if n >= 2:
                    inverse_deviation(4, n - 2, s.moments4, s.rstd4)

            pool.wait_ge(s.zeroed, 32)
            pool.wait_ge(s.xn4_ready, NB)
            pool.wait_ge(s.r_slots_ready, 2)
            for n in range(NB):
                nc.gpsimd.indirect_dma_start(
                    out=xe_dram, out_offset=bass.IndirectOffsetOnAxis(ap=slots1[:, n:n + 1], axis=0),
                    in_=rows_sb[:, n * C:(n + 1) * C], in_offset=None).then_inc(s.r_scattered, 16)
            after(pool, s.y1_even, 16 * (NE // 2 + 1))
            after(pool, s.y1_odd, 16 * (NE // 2 + 1))
            for n in range(NB):
                nc.gpsimd.indirect_dma_start(
                    out=z_sb[:, n * C:(n + 1) * C], out_offset=None, in_=ye_dram,
                    in_offset=bass.IndirectOffsetOnAxis(ap=slots1[:, NB + n:NB + n + 1], axis=0)
                ).then_inc((s.z_first, s.z_second)[n // (NB // 2)], 16)

        @block.scalar
        def _(act):
            def copy(out, in_):
                return nc.scalar.copy(out, in_)

            act.dma_start(x_sb[:, 0:C], x_d[:, 0:C]).then_inc(s.x0_in, 16)
            act.dma_start(consts[:, :], consts_d).then_inc(s.consts_in, 16)

            for counted in (s.nrmT_ready, s.xn4T_ready):
                act.sem_inc(counted, 1)
            for counted in (s.y_even, s.y_odd, s.y1_even, s.y1_odd):
                act.sem_inc(counted, 16)

            def part_of_logits(part, bank_no, done, copied):
                lo, hi = [n * TOK for n in LOGIT_PARTS[part]]
                after(act, done, part + 1)
                copy(logitsT[:, lo:hi], bank(bank_no, hi - lo, NE)).then_inc(copied, 1)

            def keys_of_layer1(a, g, bank_no):
                if isinstance(a.n, int) and a.n == 0:
                    after(act, s.wx_in, 32)
                after(act, s.keys2_done, KC * a.n + (2 if g == 0 else 1))
                nc.scalar.activation(keys2[:, g * KEYS:(g + 1) * KEYS], bank(bank_no, KEYS), ACT.Identity,
                                     bias=bx[:, g:g + 1]).then_inc(s.keys2_copied, 1)

            def beat_a(a, b, c, d):
                if a:
                    after(act, s.xn_transposed, a.n + 1)
                    after(act, s.kq_done, a.n)
                    copy(split(xnT, KC)[:, :, 0:TOK], split(bank(4, KC * TOK), KC)).then_inc(s.xnT_ready, 1)
                if c:
                    after(act, s.o_transposed, c.n + 1)
                    if not a:
                        after(act, s.proj_done, c.n)
                    copy(oT, bank(5, KC * TOK)).then_inc(s.oT_ready, 1)
                if a:
                    after(act, s.keys2_stored, 16 * a.n)
                    keys_of_layer1(a, 1, 7)
                if b:
                    after(act, s.q_transposed, b.n + 1)
                    after(act, s.attn_done, b.n)
                    copy(qT, bank(5, KC * TOK)).then_inc(s.qT_ready, 1)
                if a:
                    after(act, s.v_done, a.n + 1)
                    if c:
                        after(act, s.proj_done, c.n + 1)
                    after(act, s.vr_ready, a.n)
                    copy(v_sb, bank(2, KCH * C, KR)).then_inc(s.v_copied, 1)
                    keys_of_layer1(a, 0, 6)
                if d and not c:
                    part_of_logits(1, 1, s.logitsT_done, s.logitsT_copied)
                if d:
                    after(act, s.nrm_ready, d.n + 1)
                    copy(row(rows_sb, d.n), nrm).then_inc(s.nrm_kept, 1)
                    after(act, s.nrm_transposed, d.n + 1)
                    copy(split(rowsT[:, :], KC)[:, :, ds(d.n * TOK, TOK)], split(bank(4, KC * TOK), KC)).then_inc(s.nrmT_ready, 1)
                if a:
                    after(act, s.kq_centered, a.n + 1)
                    after(act, s.kv_done, a.n)
                    after(act, s.q_ready, a.n)
                    nc.scalar.activation(kqe, kq, ACT.Exp).then_inc(s.kq_exp, 1)
                if b and not a:
                    part_of_logits(0, 0, s.logitsT_done, s.logitsT_copied)

            run_beats(act, beat_a)

            part_of_logits(2, 0, s.logitsT_done, s.logitsT_copied)
            act.wait_ge(s.centred, 1)
            nc.scalar.activation(be["exp"][:, :], be["cent"][:, :], ACT.Exp).then_inc(s.exponentials, 1)
            act.wait_ge(s.gap, 1)
            nc.scalar.activation(tb["egap"][:, :], tb["gap"][:, :], ACT.Exp).then_inc(s.gap_exp, 1)
            act.wait_ge(s.nrm_kept, NB)
            for m, h in enumerate(SHARED_ORDER):
                for g in range(KC):
                    after(act, s.sh_up_done, KC * m + g + 1)
                    after(act, s.sh_hid, KC * (m - 1) + g + 1)
                    nc.scalar.activation(sh_sg[:, g * HT:(g + 1) * HT], bank(4 * h + 2 * g, HT), ACT.Silu).then_inc(s.sh_silu, 1)

            def tile(i, last):
                for j3 in range(3):
                    after(act, s.gu_done, 3 * i.n + j3 + 1)
                    after(act, s.h_ready, 3 * i.n + j3 - 2)
                    nc.scalar.activation(sg[:, j3 * C:(j3 + 1) * C], bank(j3, C), ACT.Silu).then_inc(s.silu_done, 1)
                if last:
                    result(last)
                after(act, s.h_transposed, 2 * i.n + 2)
                after(act, s.down_done, i.n)
                copy(hT[:, FF0 // 2:], bank(4, FF0 // 2)).then_inc(s.hT_hi, 1)

            def result(i):
                stored = (s.y_even, s.y_odd)[i.half]
                after(act, s.down_done, i.n + 1)
                after(act, stored, 16 * (i.pair + 1))
                copy(y_sb[i.half], bank(5, C)).then_inc(s.y_copied, 1)
                act.wait_ge(s.y_copied, i.n + 1)
                act.dma_start(yg_dram[ds(i.n * P, P), :], y_sb[i.half]).then_inc(stored, 16)

            tile(beat(0, 0), None)
            with act.Fori(0, TILES // 2 - 1, 1) as j:
                for k in range(1, 3):
                    tile(beat(j, k), beat(j, k - 1))
            tile(beat(0, TILES - 1), beat(0, TILES - 2))
            result(beat(0, TILES - 1))

            def beat_c(a, b, c):
                if a:
                    after(act, s.xn3_transposed, a.n + 1)
                    copy(xn3T, bank(4, KC * TOK)).then_inc(s.xn3T_ready, 1)
                    after(act, s.q1_done, a.n + 1)
                    after(act, s.score_done, a.n)
                    for g in range(KC):
                        nc.scalar.activation(q1T[:, g * TOK:(g + 1) * TOK], bank(5, TOK, at=g * TOK), ACT.Identity,
                                             bias=bx[:, g:g + 1]).then_inc(s.q1T_ready, 1)
                if b:
                    after(act, s.p_transposed, b.n + 1)
                    after(act, s.av_done, b.n)
                    full = (KCH - 1) * TOK
                    copy(pT[:, 0:full], bank(1, full, KR))
                    copy(pT[0:KLAST, full:], bank(1, TOK, KLAST, at=full)).then_inc(s.pT_ready, 1)
                if a:
                    after(act, s.vT_done, a.n + 1)
                    full = (KCH - 1) * C
                    copy(v_nat[a.half][:, 0:full], bank(2, full, KR))
                    copy(v_nat[a.half][0:KLAST, full:], bank(2, C, KLAST, at=full)).then_inc(s.vn_ready, 1)
                if a:
                    after(act, s.neg_max, a.n + 1)
                    after(act, s.p_recip, a.n)
                    nc.scalar.activation(p_sb[:, 0:KEYS], bank(6, KEYS, TOK), ACT.Exp, bias=p_neg[:, :], scale=1.0 / math.sqrt(C),
                                         accum_out=p_sum[:, :]).then_inc(s.p_ready, 1)
                if c and not b:
                    part_of_logits(1, 6, s.r_logitsT_done, s.r_logitsT_copied)
                if c:
                    after(act, s.xn4_made, c.n + 1)
                    copy(row(rows_sb, c.n), xn4).then_inc(s.xn4_ready, 1)
                    after(act, s.xn4_transposed, c.n + 1)
                    copy(split(rowsT[:, :], KC)[:, :, ds(c.n * TOK, TOK)], split(bank(0, KC * TOK), KC)).then_inc(s.xn4T_ready, 1)
                if b and not a:
                    part_of_logits(0, 5, s.r_logitsT_done, s.r_logitsT_copied)

            run_beats_c(act, beat_c)

            part_of_logits(2, 5, s.r_logitsT_done, s.r_logitsT_copied)
            act.wait_ge(s.r_centred, 1)
            nc.scalar.activation(be["exp"][:, :], be["cent"][:, :], ACT.Exp).then_inc(s.r_exponentials, 1)
            act.wait_ge(s.small_in, 16 * 4)

            def expert(e, last):
                for j8 in range(FC1):
                    after(act, s.up1_done, FC1 * e.n + j8 + 1)
                    after(act, s.down1_done, e.n)
                    nc.scalar.activation(hidT[:, j8 * CAP:(j8 + 1) * CAP], bank(j8 % 3, CAP), ACT.Gelu,
                                         bias=b1[:, ds(e.n * FC1 + j8, 1)]).then_inc(s.gelu_done, 1)
                if last:
                    result1(last)

            def result1(e):
                stored = (s.y1_even, s.y1_odd)[e.half]
                after(act, s.yT_transposed, e.n + 1)
                after(act, stored, 16 * (e.pair + 1))
                copy(y1[e.half], bank(6, 2 * C, HALF)).then_inc(s.y1_copied, 1)
                act.wait_ge(s.y1_copied, e.n + 1)
                act.dma_start(ye_dram[ds(e.n * CAP, CAP), :].rearrange("(m p) c -> p m c", p=HALF),
                              split(y1[e.half], 2)).then_inc(stored, 16)

            expert(beat(0, 0), None)
            with act.Fori(0, NE // 2 - 1, 1) as j:
                for k in range(1, 3):
                    expert(beat(j, k), beat(j, k - 1))
            expert(beat(0, NE - 1), beat(0, NE - 2))
            result1(beat(0, NE - 1))

        @block.vector
        def _(dve):
            def tt(out, a, b, op):
                return nc.vector.tensor_tensor(out, a, b, op)

            def reduce(out, in_, op):
                return nc.vector.tensor_reduce(out, in_, AX.X, op)

            def moments(kind, b, src, steps):
                nc.vector.bn_stats(bn[kind][:, :], src).then_inc(steps, 1)
                after_alone(dve, steps, MOMENTS * b.n + 1)
                nc.vector.bn_aggr(mv[kind][:, :], bn[kind][:, :]).then_inc(steps, 1)
                dve.wait_ge(steps, MOMENTS * b.n + 2)
                nc.vector.tensor_scalar(ve[kind][:, :], mv[kind][:, 1:2], EPS, None, ALU.add).then_inc(steps, 1)

            def normalise(kind, b, out, src, rstd_sem):
                dve.wait_ge(rstd_sem, b.n + 1)
                return nc.vector.tensor_scalar(out, src, mv[kind][:, 0:1], rstd[kind][:, :], ALU.subtract, ALU.mult)

            def first_norm_moments(b):
                moments(0, b, row(x_sb, b.n), s.moments0)

            def first_norm(b):
                after(dve, s.xn_transposed, b.n)
                normalise(0, b, xn, row(x_sb, b.n), s.rstd0).then_inc(s.xn_ready, 1)

            for t in ctxT:
                nc.vector.memset(split(t, KC)[:, :, KEYS:KCH * KR], 0.0).then_inc(s.zero_pad, 1)
            nc.vector.memset(split(xnT, KC)[:, :, TOK:KR], 0.0).then_inc(s.zero_pad, 1)
            for t in sums[:3]:
                nc.vector.memset(t[:, :], 0.0).then_inc(s.zero_pad, 1)
            nc.vector.memset(zero8[:, :], 0.0).then_inc(s.zero_pad, 1)
            after(dve, s.x0_in, 16)
            first_norm_moments(beat(0, 0))
            first_norm(beat(0, 0))
            after(dve, s.bias_in, 32)
            after(dve, s.consts_in, 16)
            after(dve, s.x_in, 16)

            def beat_a(a, b, c, d):
                nxt = Beat(a.n + 1, 1 - a.half, None) if a and not is_last(a) else None
                if c:
                    after(dve, s.attn_done, c.n + 1)
                    num = split(bank(7, KC * KV, TOK), KC)
                    nc.vector.reciprocal(split(den[:, :], KC), num[:, :, P:KV]).then_inc(s.den_recip, 1)
                    dve.wait_ge(s.den_recip, c.n + 1)
                    for g in range(KC):
                        tt(split(o1[:, g * P:(g + 1) * P], HG), split(num[:, g, 0:P], HG),
                           each(den[:, g * HG:(g + 1) * HG], HD), ALU.mult).then_inc(s.attn_scaled, 1)
                    after(dve, s.q_plus_bv, c.n + 1)
                    dve.wait_ge(s.attn_scaled, KC * (c.n + 1))
                    tt(o_sb, o1, q_bv, ALU.add).then_inc(s.o_ready, 1)
                if b:
                    after(dve, s.kq_exp, b.n + 1)
                    reduce(kq_s[:, :], split(kqe, 4 * HEADS), ALU.add).then_inc(s.kq_sum, 1)
                    dve.wait_ge(s.kq_sum, b.n + 1)
                    after(dve, s.q_ready, b.n)
                    nc.vector.reciprocal(kq_r[:, :], kq_s[:, :]).then_inc(s.kq_recip, 1)
                    dve.wait_ge(s.kq_recip, b.n + 1)
                    after(dve, s.v_copied, b.n + 1)
                    after(dve, s.kv_done, b.n)
                    vr_v = vr.rearrange("p (c g n) -> p c g n", c=KCH, g=KC)
                    for g in range(KC):
                        per_head = split(kq_r[:, 0:KCH * HEADS], KCH)[:, :, g * HG:(g + 1) * HG]
                        tt(vr_v[:, :, g, 0:P].rearrange("p c (h d) -> p c h d", h=HG),
                           split(v_sb, KCH)[:, :, g * P:(g + 1) * P].rearrange("p c (h d) -> p c h d", h=HG),
                           per_head.unsqueeze(3).to_broadcast([KR, KCH, HG, HD]), ALU.mult)
                        last = nc.vector.tensor_copy(vr_v[:, :, g, P:KV], per_head)
                    last.then_inc(s.vr_ready, 1)
                if d:
                    normalise(1, d, n1, row(x_sb, d.n), s.rstd1).then_inc(s.n1_ready, 1)
                    dve.wait_ge(s.n1_ready, d.n + 1)
                    moments(2, d, n1, s.moments2)
                if nxt:
                    first_norm_moments(nxt)
                if b:
                    after(dve, s.kv_done, b.n + 1)
                    tt(kvm, bank(6, KC * KV), const("headmask"), ALU.mult).then_inc(s.kvm_ready, 1)
                if d:
                    after(dve, s.nrm_ready, d.n)
                    normalise(2, d, n2, n1, s.rstd2).then_inc(s.n2_ready, 1)
                if a:
                    after(dve, s.kq_done, a.n + 1)
                    tt(kq, bank(0, 4 * C, KR), bias4[0:KR, :], ALU.add).then_inc(s.kq_biased, 1)
                    dve.wait_ge(s.kq_biased, a.n + 1)
                    reduce(kq_m[:, :], split(kq, 4 * HEADS), ALU.max).then_inc(s.kq_max, 1)
                if c:
                    after(dve, s.proj_done, c.n + 1)
                    after(dve, s.x_plus_bp, c.n + 1)
                    if a:
                        after(dve, s.v_copied, a.n + 1)
                    tt(row(x_sb, c.n), bank(3, C, TOK, at=C), xbp, ALU.add).then_inc(s.x1_ready, 1)
                    after_alone(dve, s.x1_ready, c.n + 1)
                    moments(1, c, row(x_sb, c.n), s.moments1)
                if nxt:
                    first_norm(nxt)

            run_beats(dve, beat_a)

            steps = [0]

            def then(ins):
                steps[0] += 1
                ins.then_inc(s.routing_step, 1)
                dve.wait_ge(s.routing_step, steps[0])

            def by_token(n):
                return split(be[n][:, :], NB)

            def probabilities(logits_sem, centred, exponentials):
                after(dve, logits_sem, 1)
                logits = split(bank(2, NB * NE, TOK), NB)
                then(reduce(tb["max"][:, :], logits, ALU.max))
                tt(by_token("cent"), logits, each(tb["max"][:, :], NE), ALU.subtract).then_inc(centred, 1)
                after(dve, exponentials, 1)
                then(reduce(tb["sum"][:, :], by_token("exp"), ALU.add))
                then(nc.vector.reciprocal(tb["rec"][:, :], tb["sum"][:, :]))
                then(tt(by_token("probs"), by_token("exp"), each(tb["rec"][:, :], NE), ALU.mult))

            expert_m = split(const("expert_m", TOK), NB)

            def first_largest(src, top, hot):
                then(reduce(tb[top][:, :], by_token(src), ALU.max))
                then(tt(by_token("eq"), by_token(src), each(tb[top][:, :], NE), ALU.is_equal))
                then(tt(by_token("eqm"), by_token("eq"), expert_m, ALU.mult))
                then(reduce(tb["idx"][:, :], by_token("eqm"), ALU.min))
                then(tt(by_token(hot), expert_m, each(tb["idx"][:, :], NE), ALU.is_equal))

            def sum_batches():
                for w in range(3):
                    last = tt(blocks(w + 1, PAD, NB + 1), blocks(w, PAD, NB + 1), blocks(w, PAD - (1 << w), NB + 1), ALU.add)
                    if w < 2:
                        then(last)
                return last

            probabilities(s.logits_done, s.centred, s.exponentials)
            first_largest("probs", "top1", "hot1")
            then(nc.vector.scalar_tensor_tensor(be["masked"][:, :], be["hot1"][:, :], -4.0, be["probs"][:, :], ALU.mult, ALU.add))
            first_largest("masked", "top2", "hot2")
            then(tt(hots[:, 0:NB * NE], be["hot1"][:, :], be["hot2"][:, :], ALU.add))
            sum_batches().then_inc(s.both_hot, 1)
            tt(tb["gap"][:, :], tb["top2"][:, :], tb["top1"][:, :], ALU.subtract).then_inc(s.gap, 1)
            after(dve, s.gap_exp, 1)
            then(nc.vector.tensor_scalar(tb["gden"][:, :], tb["egap"][:, :], 1.0, None, ALU.add))
            then(nc.vector.reciprocal(tb["g1"][:, :], tb["gden"][:, :]))
            then(tt(tb["g2"][:, :], tb["egap"][:, :], tb["g1"][:, :], ALU.mult))
            after(dve, s.rank_done, 1)
            nc.vector.tensor_copy(rank[:, :], bank(3, (NB + 1) * NE)).then_inc(s.rank_copied, 1)
            dve.wait_ge(s.rank_copied, 1)
            then(tt(split(over_edge[:, :], NE), each(rank[:, NB * NE:], TILES // 2), split(const("tile_edge"), NE), ALU.is_gt))
            then(reduce(tiles_n[:, :], split(over_edge[:, :], NE), ALU.add))
            then(nc.vector.tensor_tensor_scan(tiles_scan[:, :], tiles_n[:, :], zero8[:, :], 0.0, ALU.add, ALU.add))
            then(tt(first_tile[:, :], tiles_scan[:, :], tiles_n[:, :], ALU.subtract))
            then(nc.vector.tensor_scalar(base_row[:, :], first_tile[:, :], float(P), None, ALU.mult))
            then(tt(by_token("rows"), split(rank[0:TOK, 0:NB * NE], NB),
                    base_row[0:TOK, :].unsqueeze(1).to_broadcast([TOK, NB, NE]), ALU.add))
            for k, (hot, pick, slot) in enumerate((("hot1", "pick1", "slot1"), ("hot2", "pick2", "slot2"))):
                then(tt(be[pick][:, :], be["rows"][:, :], be[hot][:, :], ALU.mult))
                then(reduce(tb[slot][:, :], by_token(pick), ALU.add))
                nc.vector.tensor_copy(slots0[:, k * NB:(k + 1) * NB], tb[slot][:, :]).then_inc(s.slots_ready, 1)
            then(tt(split(tile_cmp[:, :], TILES), each(const("tile_no", 1), NE),
                    tiles_scan[0:1, :].unsqueeze(1).to_broadcast([1, TILES, NE]), ALU.is_ge))
            then(reduce(tile_expert[:, :], split(tile_cmp[:, :], TILES), ALU.add))
            nc.vector.tensor_scalar(tile_off[:, :], tile_expert[:, :], float(NE - 1), float(EW), ALU.min, ALU.mult).then_inc(s.tile_off, 1)

            for m, h in enumerate(SHARED_ORDER):
                for g in range(KC):
                    after(dve, s.sh_silu, KC * m + g + 1)
                    tt(sh_hT[:, g * NT + h * HT:g * NT + (h + 1) * HT], sh_sg[:, g * HT:(g + 1) * HT],
                       bank(4 * h + 2 * g + 1, HT), ALU.mult).then_inc(s.sh_hid, 1)
            for n in range(NB):
                after(dve, s.sh_down_done, n + 1)
                tt(row(x_sb, n), bank(n % 4, C, TOK), row(x_sb, n), ALU.add).then_inc(s.x1s_ready, 1)

            def next_rows(i):
                after(dve, s.xg_transposed, i.n + 1)
                after(dve, s.gu_done, 3 * i.n)
                nc.vector.tensor_copy(xgT, bank(6, KC * P)).then_inc(s.xgT_ready, 1)

            def tile(i, nxt):
                after(dve, s.h_transposed, 2 * i.n)
                for j3 in range(3):
                    after(dve, s.silu_done, 3 * i.n + j3 + 1)
                    tt(h_sb[:, j3 * C:(j3 + 1) * C], sg[:, j3 * C:(j3 + 1) * C], bank(j3, C, at=C), ALU.mult).then_inc(s.h_ready, 1)
                if nxt:
                    next_rows(nxt)
                after(dve, s.h_transposed, 2 * i.n + 1)
                after(dve, s.down_done, i.n)
                nc.vector.tensor_copy(hT[:, 0:FF0 // 2], bank(3, FF0 // 2)).then_inc(s.hT_lo, 1)

            next_rows(beat(0, 0))
            tile(beat(0, 0), beat(0, 1))
            with dve.Fori(0, TILES // 2 - 1, 1) as j:
                for k in range(1, 3):
                    tile(beat(j, k), beat(j, k + 1))
            tile(beat(0, TILES - 1), None)

            def combine(n, y):
                nc.vector.scalar_tensor_tensor(row(x_sb, n.n), y[:, 0:C], tb["g1"][:, ds(n.n, 1)], row(x_sb, n.n),
                                               ALU.mult, ALU.add).then_inc(s.comb1, 1)
                dve.wait_ge(s.comb1, n.n + 1)
                nc.vector.scalar_tensor_tensor(row(x_sb, n.n), y[:, C:2 * C], tb["g2"][:, ds(n.n, 1)], row(x_sb, n.n),
                                               ALU.mult, ALU.add).then_inc(s.x2_ready, 1)
                after_alone(dve, s.x2_ready, n.n + 1)
                moments(3, n, row(x_sb, n.n), s.moments3)

            def third_norm(n):
                after(dve, s.xn3_transposed, n.n)
                normalise(3, n, xn3, row(x_sb, n.n), s.rstd3).then_inc(s.xn3_ready, 1)

            def beat_c(t):
                a, b, c = [beat(0, t - back) if 0 <= t - back < NB else None for back in range(3)]
                nxt = beat(0, t + 1) if t + 1 < NB else None
                if b:
                    after(dve, s.p_ready, b.n + 1)
                    nc.vector.reciprocal(p_rec[:, :], p_sum[:, :]).then_inc(s.p_recip, 1)
                if nxt:
                    after(dve, (s.yg_0, s.yg_1, s.yg_2, s.yg_3)[nxt.n % YG], 32 * (nxt.n // YG + 1))
                    combine(nxt, yg[nxt.n % YG])
                if c:
                    after(dve, s.xn4T_ready, c.n + 1)
                    normalise(4, c, xn4, row(x_sb, c.n), s.rstd4).then_inc(s.xn4_made, 1)
                if nxt:
                    third_norm(nxt)
                if a:
                    after(dve, s.score_done, a.n + 1)
                    reduce(p_max[:, :], bank(6, KEYS, TOK), ALU.max).then_inc(s.score_max, 1)
                    dve.wait_ge(s.score_max, a.n + 1)
                    nc.vector.tensor_scalar(p_neg[:, :], p_max[:, :], -1.0 / math.sqrt(C), None, ALU.mult).then_inc(s.neg_max, 1)
                if b:
                    dve.wait_ge(s.p_recip, b.n + 1)
                    after(dve, s.av_done, b.n + 1)
                    nc.vector.scalar_tensor_tensor(row(x_sb, b.n), bank(7, C, TOK), p_rec[:, :], row(x_sb, b.n),
                                                   ALU.mult, ALU.add).then_inc(s.x3_ready, 1)
                    after_alone(dve, s.x3_ready, b.n + 1)
                    moments(4, b, row(x_sb, b.n), s.moments4)

            after(dve, s.yg_0, 32)
            combine(beat(0, 0), yg[0])
            third_norm(beat(0, 0))
            for t in range(NB + 2):
                beat_c(t)

            probabilities(s.r_logits_done, s.r_centred, s.r_exponentials)
            first_largest("probs", "top1", "hot1")
            then(nc.vector.tensor_copy(hots[:, 0:NB * NE], be["hot1"][:, :]))
            sum_batches().then_inc(s.r_hots, 1)
            then(tt(be["pick2"][:, :], be["hot1"][:, :], const("cap_base", TOK), ALU.mult))
            then(reduce(tb["base"][:, :], by_token("pick2"), ALU.add))
            after(dve, s.r_rank_done, 1)
            tt(be["pick1"][:, :], be["hot1"][:, :], bank(3, NB * NE, TOK), ALU.mult).then_inc(s.r_pick, 1)
            dve.wait_ge(s.r_pick, 1)
            then(reduce(tb["pos"][:, :], by_token("pick1"), ALU.add))
            then(nc.vector.tensor_scalar(tb["kept"][:, :], tb["pos"][:, :], float(CAP), None, ALU.is_lt))
            then(tt(tb["raw"][:, :], tb["base"][:, :], tb["pos"][:, :], ALU.add))
            then(tt(tb["rel"][:, :], tb["raw"][:, :], const("spare_row", TOK), ALU.subtract))
            then(tt(tb["relk"][:, :], tb["rel"][:, :], tb["kept"][:, :], ALU.mult))
            tt(slots1[:, 0:NB], tb["relk"][:, :], const("spare_row", TOK), ALU.add).then_inc(s.r_slots_ready, 1)
            nc.vector.scalar_tensor_tensor(slots1[:, NB:], tb["pos"][:, :], float(CAP - 1), tb["base"][:, :],
                                           ALU.min, ALU.add).then_inc(s.r_slots_ready, 1)
            then(tt(tb["w"][:, :], tb["top1"][:, :], tb["kept"][:, :], ALU.mult))

            def next_rows1(e):
                after(dve, s.xe_transposed, e.n + 1)
                after(dve, s.up1_done, FC1 * e.n)
                nc.vector.tensor_copy(xeT, bank(5, KC * CAP)).then_inc(s.xeT_ready, 1)

            def down1(e):
                after(dve, s.down1_done, e.n + 1)
                for g in range(KC):
                    nc.vector.tensor_scalar(yT[:, g * CAP:(g + 1) * CAP], bank(3 + g, CAP), b2[:, ds(e.n * KC + g, 1)], None,
                                            ALU.add).then_inc(s.yT_ready, 1)

            dve.wait_ge(s.small_in, 16 * 4)
            next_rows1(beat(0, 0))
            with dve.Fori(0, NE - 1, 1) as j:
                e, nxt = Beat(j, 0, 0), Beat(j + 1, 0, 0)
                next_rows1(nxt)
                down1(e)
            down1(beat(0, NE - 1))
            for n in range(NB):
                after(dve, (s.z_first, s.z_second)[n // (NB // 2)], 16 * (NB // 2))
                nc.vector.scalar_tensor_tensor(row(x_sb, n), z_sb[:, n * C:(n + 1) * C], tb["w"][:, n:n + 1], row(x_sb, n),
                                               ALU.mult, ALU.add).then_inc(s.out_ready, 1)

        @block.tensor
        def _(pe):
            mm, tr = nc.tensor.matmul, nc.tensor.transpose

            def weight(n, k):
                return proj_w[:, (n * KC + k) * C:(n * KC + k + 1) * C]

            def keys(half, k, c):
                return split(ctxT[half], KC)[:, k, c * KR:(c + 1) * KR]

            def transpose_rows(bank_no, src, rows=TOK):
                for g in range(KC):
                    last = tr(bank(bank_no, rows, at=g * rows), src[:, g * P:(g + 1) * P], ident[0:rows, 0:rows])
                return last

            pe.wait_ge(s.zero_pad, 7)
            pe.wait_ge(s.wk_in, 16)

            def part_of_logits(which, part, bank_no, done):
                lo, hi = [n * TOK for n in LOGIT_PARTS[part]]
                for k in range(KC):
                    last = mm(bank(bank_no, hi - lo, NE), routers[:, (which * KC + k) * NE:(which * KC + k + 1) * NE],
                              rowsT[:, k * NT + lo:k * NT + hi], start=k == 0, stop=k == KC - 1)
                last.then_inc(done, 1)

            def logits(copied, done):
                after(pe, copied, 3)
                for n in range(NB):
                    last = tr(bank(2, NE, TOK, at=n * NE), logitsT[:, n * TOK:(n + 1) * TOK], ident[0:NE, 0:NE])
                last.then_inc(done, 1)

            def values(a, c3):
                for k in range(KC):
                    last = mm(bank(2, C, KR, at=c3 * C), keys(a.half, k, c3), weight(2, k), start=k == 0, stop=k == KC - 1)
                return last

            def keys_of_layer1(a, g, bank_no):
                if isinstance(a.n, int) and a.n == 0:
                    after(pe, s.wx_in, 32)
                for k in range(KC):
                    last = mm(bank(bank_no, KEYS), wx_a[:, k * C + g * P:k * C + (g + 1) * P],
                              split(ctxT[a.half], KC)[:, k, 0:KEYS], start=k == 0, stop=k == KC - 1)
                last.then_inc(s.keys2_done, 1)

            def beat_a(a, b, c, d):
                if a:
                    after(pe, ctx_half(a), 16 * (a.pair + 1))
                    after(pe, s.kq_biased, a.n)
                    for c3 in range(KCH):
                        for k in range(KC):
                            mm(bank(0, C, KR, at=c3 * C), keys(a.half, k, c3), weight(1, k), start=k == 0, stop=k == KC - 1)
                    after(pe, s.xn_ready, a.n + 1)
                    if isinstance(a.n, int):
                        after(pe, s.attn_w_in, 32)
                        after(pe, s.consts_in, 16)
                        if a.n >= 4:
                            after(pe, s.nrmT_ready, a.n - 2)
                    else:
                        after(pe, s.nrmT_ready, a.n - 2)
                    transpose_rows(4, xn).then_inc(s.xn_transposed, 1)
                    after(pe, s.v_copied, a.n)
                    values(a, 0)
                if c:
                    after(pe, s.o_ready, c.n + 1)
                    after(pe, s.qT_ready, c.n + 1)
                    transpose_rows(5, o_sb).then_inc(s.o_transposed, 1)
                if a:
                    after(pe, s.xnT_ready, a.n + 1)
                    for k in range(KC):
                        last = mm(bank(0, C, KR, at=KCH * C), xnT[:, k * KR:(k + 1) * KR], weight(0, k), start=k == 0, stop=k == KC - 1)
                    last.then_inc(s.kq_done, 1)
                    values(a, 1)
                    if c:
                        after(pe, s.attn_scaled, KC * (c.n + 1))
                    keys_of_layer1(a, 1, 7)
                if c:
                    after(pe, s.x1_ready, c.n)
                    after(pe, s.oT_ready, c.n + 1)
                    for k in range(KC):
                        last = mm(bank(3, C, TOK, at=C), oT[:, k * TOK:(k + 1) * TOK], weight(3, k), start=k == 0, stop=k == KC - 1)
                    last.then_inc(s.proj_done, 1)
                if b:
                    after(pe, s.vr_ready, b.n + 1)
                    after(pe, s.keys2_copied, KC * (b.n + 1))
                    for g in range(KC):
                        for c3 in range(KCH):
                            rows = KR if c3 < KCH - 1 else KLAST
                            last = mm(bank(6, KV, at=g * KV), kqe[0:rows, c3 * C + g * P:c3 * C + (g + 1) * P],
                                      vr[0:rows, (c3 * KC + g) * KV:(c3 * KC + g + 1) * KV], start=c3 == 0, stop=c3 == KCH - 1)
                    last.then_inc(s.kv_done, 1)
                    after(pe, s.q_ready, b.n + 1)
                    after(pe, s.oT_ready, b.n)
                    transpose_rows(5, q_sb).then_inc(s.q_transposed, 1)
                if a:
                    values(a, 2).then_inc(s.v_done, 1)
                if b:
                    after(pe, s.kvm_ready, b.n + 1)
                if a:
                    keys_of_layer1(a, 0, 6)
                if b:
                    after(pe, s.qT_ready, b.n + 1)
                    if a:
                        after(pe, s.keys2_copied, KC * a.n + 1)
                    after(pe, s.attn_scaled, KC * b.n)
                    for g in range(KC):
                        last = mm(bank(7, KV, TOK, at=g * KV), qT[:, g * TOK:(g + 1) * TOK], kvm[:, g * KV:(g + 1) * KV], start=True, stop=True)
                    last.then_inc(s.attn_done, 1)
                if d and not c:
                    after(pe, s.nrmT_ready, NB)
                    part_of_logits(0, 1, 1, s.logitsT_done)
                if d:
                    after(pe, s.nrm_ready, d.n + 1)
                    after(pe, s.xnT_ready, min(d.n + 4, NB) if isinstance(d.n, int) else d.n + 4)
                    if not a:
                        after(pe, s.nrmT_ready, d.n + 1)
                    transpose_rows(4, nrm).then_inc(s.nrm_transposed, 1)
                if b and not a:
                    after(pe, s.small_in, 16 * 4)
                    part_of_logits(0, 0, 0, s.logitsT_done)

            run_beats(pe, beat_a)

            def ranks(done):
                mm(bank(3, (NB + 1) * NE), const("ones", TOK), blocks(3, PAD, NB + 1), start=True, stop=False)
                last = mm(bank(3, (NB + 1) * NE), const("earlier", TOK), hots, start=False, stop=True)
                last.then_inc(done, 1)

            after(pe, s.nrmT_ready, NB + 1)
            part_of_logits(0, 2, 0, s.logitsT_done)
            logits(s.logitsT_copied, s.logits_done)

            def shared_up(h):
                for g in range(KC):
                    for part in range(2):
                        o = bank(4 * h + 2 * g + part, HT)
                        for k in range(KC):
                            at = k * 2 * FFS + part * FFS + g * P
                            last = mm(o, shared_w[:, at:at + P], rowsT[:, k * NT + h * HT:k * NT + (h + 1) * HT], start=k == 0, stop=k == KC - 1)
                    last.then_inc(s.sh_up_done, 1)

            shared_up(SHARED_ORDER[0])
            after(pe, s.both_hot, 1)
            ranks(s.rank_done)
            after(pe, s.rank_copied, 1)
            shared_up(SHARED_ORDER[1])
            for n in range(NB):
                after(pe, s.sh_hid, 2 * KC)
                after(pe, s.x1s_ready, n - 3)
                for k in range(KC):
                    last = mm(bank(n % 4, C, TOK), sh_hT[:, k * NT + n * TOK:k * NT + (n + 1) * TOK],
                              shared_w[:, KC * 2 * FFS + k * C:KC * 2 * FFS + (k + 1) * C], start=k == 0, stop=k == KC - 1)
                last.then_inc(s.sh_down_done, 1)

            def rows_in(i):
                after(pe, (s.xg_even, s.xg_odd)[i.half], 16 * (i.pair + 1))
                after(pe, s.xgT_ready, i.n)
                transpose_rows(6, xg[i.half], P).then_inc(s.xg_transposed, 1)

            def gate_up(i):
                off = pe.value_load(tile_off[0:1, ds(i.n, 1)], min_val=0, max_val=(NE - 1) * EW)
                after(pe, s.xgT_ready, i.n + 1)
                for j3 in range(3):
                    after(pe, s.h_ready, 3 * i.n + j3 - 2)
                    for k in range(KC):
                        last = mm(bank(j3), xgT[:, k * P:(k + 1) * P], wres[:, ds(off + (k * GU + j3 * BANK), BANK)], start=k == 0, stop=k == KC - 1)
                    last.then_inc(s.gu_done, 1)
                return off

            def down(i):
                off = pe.value_load(tile_off[0:1, ds(i.n, 1)], min_val=0, max_val=(NE - 1) * EW)
                after(pe, s.hT_lo, i.n + 1)
                after(pe, s.hT_hi, i.n + 1)
                for k in range(FC0):
                    last = mm(bank(5, C), hT[:, k * P:(k + 1) * P], wres[:, ds(off + (KC * GU + k * C), C)], start=k == 0, stop=k == FC0 - 1)
                last.then_inc(s.down_done, 1)

            def transpose_hidden(i):
                for half in range(2):
                    after(pe, (s.hT_lo, s.hT_hi)[half], i.n)
                    for m in range(FC0 // 2):
                        k = half * (FC0 // 2) + m
                        after(pe, s.h_ready, 3 * i.n + k // 2 + 1)
                        last = tr(bank(3 + half, P, at=m * P), h_sb[:, k * P:(k + 1) * P], ident)
                    last.then_inc(s.h_transposed, 1)

            after(pe, s.tile_off, 1)
            after(pe, s.experts_in, 16 * NE)
            after(pe, s.x1s_ready, NB)
            rows_in(beat(0, 0))
            gate_up(beat(0, 0))
            rows_in(beat(0, 1))
            transpose_hidden(beat(0, 0))
            with pe.Fori(0, TILES // 2 - 1, 1) as j:
                for k in range(1, 3):
                    gate_up(beat(j, k))
                    rows_in(beat(j, k + 1))
                    down(beat(j, k - 1))
                    transpose_hidden(beat(j, k))
            gate_up(beat(0, TILES - 1))
            down(beat(0, TILES - 2))
            transpose_hidden(beat(0, TILES - 1))
            down(beat(0, TILES - 1))

            after(pe, s.wx_back, 16)

            def beat_c(a, b, c):
                if a:
                    after(pe, s.xn3_ready, a.n + 1)
                    transpose_rows(4, xn3).then_inc(s.xn3_transposed, 1)
                    after(pe, (s.kT_even, s.kT_odd)[a.half], 16 * (a.pair + 1))
                    after(pe, s.vn_ready, a.n)
                    for c3 in range(KCH):
                        rows = KR if c3 < KCH - 1 else KLAST
                        for g in range(KC):
                            last = tr(bank(2, P, rows, at=c3 * C + g * P), kT[a.half][:, g * KEYS + c3 * KR:g * KEYS + c3 * KR + rows], ident)
                    last.then_inc(s.vT_done, 1)
                    after(pe, s.xn3T_ready, a.n + 1)
                    for g in range(KC):
                        for k in range(KC):
                            last = mm(bank(5, TOK, at=g * TOK), wx[:, k * C + g * P:k * C + (g + 1) * P], xn3T[:, k * TOK:(k + 1) * TOK],
                                      start=k == 0, stop=k == KC - 1)
                    last.then_inc(s.q1_done, 1)
                if b:
                    after(pe, s.p_ready, b.n + 1)
                    for c3 in range(KCH):
                        rows = KR if c3 < KCH - 1 else KLAST
                        last = tr(bank(1, TOK, rows, at=c3 * TOK), p_sb[:, c3 * KR:c3 * KR + rows], ident[0:TOK, 0:TOK])
                    last.then_inc(s.p_transposed, 1)
                if a:
                    after(pe, s.q1T_ready, KC * (a.n + 1))
                    for k in range(KC):
                        last = mm(bank(6, KEYS, TOK), q1T[:, k * TOK:(k + 1) * TOK], kT[a.half][:, k * KEYS:(k + 1) * KEYS],
                                  start=k == 0, stop=k == KC - 1)
                    last.then_inc(s.score_done, 1)
                if b:
                    after(pe, s.pT_ready, b.n + 1)
                    after(pe, s.vn_ready, b.n + 1)
                    after(pe, s.x3_ready, b.n)
                    for c3 in range(KCH):
                        rows = KR if c3 < KCH - 1 else KLAST
                        last = mm(bank(7, C, TOK), pT[0:rows, c3 * TOK:(c3 + 1) * TOK], v_nat[b.half][0:rows, c3 * C:(c3 + 1) * C],
                                  start=c3 == 0, stop=c3 == KCH - 1)
                    last.then_inc(s.av_done, 1)
                if c and not b:
                    after(pe, s.xn4T_ready, NB)
                    part_of_logits(1, 1, 6, s.r_logitsT_done)
                if c:
                    after(pe, s.xn4_made, c.n + 1)
                    after(pe, s.xn4T_ready, c.n + 1)
                    transpose_rows(0, xn4).then_inc(s.xn4_transposed, 1)
                if b and not a:
                    part_of_logits(1, 0, 5, s.r_logitsT_done)

            run_beats_c(pe, beat_c)

            after(pe, s.xn4T_ready, NB + 1)
            part_of_logits(1, 2, 5, s.r_logitsT_done)
            logits(s.r_logitsT_copied, s.r_logits_done)
            after(pe, s.r_hots, 1)
            ranks(s.r_rank_done)
            after(pe, s.r_pick, 1)

            def rows_in1(e):
                after(pe, (s.xe_even, s.xe_odd)[e.half], 16 * (e.pair + 1))
                after(pe, s.xeT_ready, e.n)
                for k in range(KC):
                    for m in range(2):
                        last = tr(bank(5, HALF, at=k * CAP + m * HALF), xe[e.half][:, m * C + k * P:m * C + (k + 1) * P], ident[0:HALF, 0:HALF])
                last.then_inc(s.xe_transposed, 1)

            def rows_out1(e):
                after(pe, s.yT_ready, KC * (e.n + 1))
                for m in range(2):
                    for g in range(KC):
                        last = tr(bank(6, P, HALF, at=m * C + g * P), yT[:, g * CAP + m * HALF:g * CAP + (m + 1) * HALF], ident)
                last.then_inc(s.yT_transposed, 1)

            def expert(e, last_e, nxt):
                after(pe, (s.w1_even, s.w1_odd)[e.half], 16 * (e.pair + 1))
                after(pe, s.xeT_ready, e.n + 1)
                for j8 in range(FC1):
                    after(pe, s.gelu_done, FC1 * e.n + j8 - 2)
                    for k in range(KC):
                        last = mm(bank(j8 % 3, CAP), w1[e.half][:, k * FF1 + j8 * P:k * FF1 + (j8 + 1) * P], xeT[:, k * CAP:(k + 1) * CAP],
                                  start=k == 0, stop=k == KC - 1)
                    last.then_inc(s.up1_done, 1)
                if last_e:
                    rows_out1(last_e)
                if nxt:
                    rows_in1(nxt)
                after(pe, (s.w2_even, s.w2_odd)[e.half], 16 * (e.pair + 1))
                after(pe, s.yT_ready, KC * e.n)
                for j8 in range(FC1):
                    after(pe, s.gelu_done, FC1 * e.n + j8 + 1)
                    for g in range(KC):
                        last = mm(bank(3 + g, CAP), w2[e.half][:, j8 * C + g * P:j8 * C + (g + 1) * P], hidT[:, j8 * CAP:(j8 + 1) * CAP],
                                  start=j8 == 0, stop=j8 == FC1 - 1)
                last.then_inc(s.down1_done, 1)

            rows_in1(beat(0, 0))
            expert(beat(0, 0), None, beat(0, 1))
            with pe.Fori(0, NE // 2 - 1, 1) as j:
                for k in range(1, 3):
                    expert(beat(j, k), beat(j, k - 1), beat(j, k + 1))
            expert(beat(0, NE - 1), beat(0, NE - 2), None)
            after(pe, s.y1_copied, NE - 1)
            rows_out1(beat(0, NE - 1))


def _chunks(w):
    k, n = w.shape
    return w.reshape(k // P, P, n).transpose(1, 0, 2).reshape(P, -1)


def kernel(**inputs):
    import numpy as _np
    import concourse.bacc as _bacc
    from concourse import mybir as _mybir
    from concourse.bass_utils import run_bass_kernel_spmd as _run

    a = {k: _np.asarray(v) for k, v in inputs.items()}
    gu = a["L0_ffn_gate_up_w"].transpose(0, 2, 1).reshape(NE, KC, P, 2, 3, C).transpose(0, 2, 1, 4, 3, 5).reshape(NE, P, KC * GU)
    dn = a["L0_ffn_down_w"].transpose(0, 2, 1).reshape(NE, FC0, P, C).transpose(0, 2, 1, 3).reshape(NE, P, FC0 * C)
    wide = lambda rows: _np.tile(_np.concatenate([a[n] for n in rows])[None, :], (P, 1))
    arrays = {
        "x": a["x"].transpose(1, 0, 2).reshape(TOK, NB * C),
        "ctx": a["ctx_1024"].transpose(0, 2, 1).reshape(NB, KC, P, KEYS).transpose(0, 2, 1, 3).reshape(NB, P, KC * KEYS),
        "proj_w": _np.concatenate([_chunks(a[n].T) for n in ("L0_xattn_Wq", "L0_xattn_Wk", "L0_xattn_Wv", "L0_xattn_Wp")], axis=1),
        "bias": wide(["L0_xattn_bk"] * KCH + ["L0_xattn_bq"]),
        "rows": wide(["L0_xattn_bv", "L0_xattn_bp", "L0_ffn_ln_gamma", "L0_ffn_ln_beta"]),
        "routers": _np.concatenate([_chunks(a["L0_ffn_router_w"].T), _chunks(a["L1_ffn_router_w"].T)], axis=1),
        "shared_w": _np.concatenate([_chunks(a["L0_ffn_shared_gate_up_w"].T), _chunks(a["L0_ffn_shared_down_w"].T)], axis=1),
        "experts": _np.concatenate([gu, dn], axis=2),
        "wx": _chunks(a["L1_xattn_W"].T),
        "bx": a["L1_xattn_b"].reshape(KC, P).T,
        "w1": a["L1_ffn_w1"].reshape(NE, KC, P, FF1).transpose(0, 2, 1, 3).reshape(NE, P, KC * FF1),
        "b1": a["L1_ffn_b1"].reshape(NE * FC1, P).T,
        "w2": a["L1_ffn_w2"].reshape(NE, FC1, P, C).transpose(0, 2, 1, 3).reshape(NE, P, FC1 * C),
        "b2": a["L1_ffn_b2"].reshape(NE * KC, P).T,
        "consts": constants(),
    }
    arrays = {k: _np.ascontiguousarray(v) for k, v in arrays.items()}
    nc = _bacc.Bacc("TRN2", target_bir_lowering=False, num_devices=1)
    args = [nc.dram_tensor("in_" + k, v.shape, _mybir.dt.from_np(v.dtype), kind="ExternalInput").ap() for k, v in arrays.items()]
    out = nc.dram_tensor("out_0", (NB, TOK, C), _mybir.dt.float32, kind="ExternalOutput").ap()
    two_layers(nc, *args, out)
    r = _run(nc, [{"in_" + k: v for k, v in arrays.items()}], core_ids=[0])
    return r.results[0]["out_0"]
```
